# Optimizing a Trainium2 kernel written in Bass

```python
import numpy as np
import jax
import jax.numpy as jnp

def _softmax(x, axis=-1):
    return jax.nn.softmax(x, axis=axis)

def _gelu(x):
    return jax.nn.gelu(x, approximate=True)

def _silu(x):
    return jax.nn.silu(x)

def _sigmoid(x):
    return jax.nn.sigmoid(x)

def _layernorm(x, axis=-1, eps=1e-05):
    m = jnp.mean(x, axis=axis, keepdims=True)
    v = jnp.var(x, axis=axis, keepdims=True)
    return (x - m) / jnp.sqrt(v + eps)

def _scatter_add(tgt, idx, src, axis=0):
    return tgt.at[idx].add(src)

def _segment_sum(src, seg, n):
    return jax.ops.segment_sum(src, seg, n)
kernel_name = 'mk_conv_seq_d1_conv_nchw256_r4_8e952e'

def setup_inputs(seed: int=0):
    np.random.seed(seed)
    _w = jnp.asarray

    def _rec_inputs():
        import jax
        import jax.numpy as jnp
        _gk = jax.random.key(seed)
        x = -0.000125 + 0.9999 * jax.random.normal(jax.random.fold_in(_gk, 1), (32, 64, 16, 16), jnp.float32)
        return x
    x = _rec_inputs()

    def _L0_conv_setup():
        import jax, jax.numpy as jnp
        from jax import lax
        import numpy as np
        WR = 7
        NH = 4
        FF = 3.0

        def _conv_bn(x, w, s, b, groups=1):
            y = lax.conv_general_dilated(x, w, (1, 1), 'SAME', dimension_numbers=('NCHW', 'OIHW', 'NCHW'), feature_group_count=groups)
            return y * s[None, :, None, None] + b[None, :, None, None]

        def _ffn(x, w1, s1, b1, w2, s2, b2):
            return _conv_bn(jax.nn.relu(_conv_bn(x, w1, s1, b1)), w2, s2, b2)

        def _focus(t):
            n0 = jnp.linalg.norm(t, axis=-1, keepdims=True)
            tp = t ** FF
            return tp / jnp.linalg.norm(tp, axis=-1, keepdims=True) * n0

        def _attn(xw, wq, wkv, pos, scale_p, dwc_w, dwc_b, proj_w, proj_b):
            Bw, N, C = xw.shape
            hd = C // NH
            q = xw @ wq.T
            kv = xw @ wkv.T
            k, v = (kv[..., :C], kv[..., C:])
            k = k + pos
            sc = jax.nn.softplus(scale_p)
            q = (jax.nn.relu(q) + 1e-06) / sc
            k = (jax.nn.relu(k) + 1e-06) / sc
            q, k = (_focus(q), _focus(k))
            heads = lambda t: t.reshape(Bw, N, NH, hd).transpose(0, 2, 1, 3).reshape(Bw * NH, N, hd)
            q, k, v = (heads(q), heads(k), heads(v))
            z = 1.0 / (jnp.einsum('bic,bc->bi', q, k.sum(axis=1)) + 1e-06)
            if N * N * (hd + hd) > hd * hd * (N + N):
                kv2 = jnp.einsum('bjc,bjd->bcd', k, v)
                y = jnp.einsum('bic,bcd,bi->bid', q, kv2, z)
            else:
                qk = jnp.einsum('bic,bjc->bij', q, k)
                y = jnp.einsum('bij,bjd,bi->bid', qk, v, z)
            num = int(round(N ** 0.5))
            fm = v.reshape(-1, num, num, hd).transpose(0, 3, 1, 2)
            fm = lax.conv_general_dilated(fm, dwc_w, (1, 1), 'SAME', dimension_numbers=('NCHW', 'OIHW', 'NCHW'), feature_group_count=hd)
            fm = fm + dwc_b[None, :, None, None]
            y = y + fm.transpose(0, 2, 3, 1).reshape(-1, N, hd)
            y = y.reshape(Bw, NH, N, hd).transpose(0, 2, 1, 3).reshape(Bw, N, C)
            return y @ proj_w.T + proj_b

        def _windowed_attn(x, wq, wkv, pos, scale_p, dwc_w, dwc_b, proj_w, proj_b):
            B, C, H, W = x.shape
            xh = x.transpose(0, 2, 3, 1)
            pb, pr = (-H % WR, -W % WR)
            xh = jnp.pad(xh, ((0, 0), (0, pb), (0, pr), (0, 0)))
            pH, pW = (H + pb, W + pr)
            nH, nW = (pH // WR, pW // WR)
            xw = xh.reshape(B, nH, WR, nW, WR, C).transpose(0, 1, 3, 2, 4, 5)
            xw = xw.reshape(B * nH * nW, WR * WR, C)
            xw = _attn(xw, wq, wkv, pos, scale_p, dwc_w, dwc_b, proj_w, proj_b)
            xh = xw.reshape(B, nH, nW, WR, WR, C).transpose(0, 1, 3, 2, 4, 5).reshape(B, pH, pW, C)
            return xh[:, :H, :W].transpose(0, 3, 1, 2)

        def _forward(x, dw0_w, dw0_s, dw0_b, f0_w1, f0_s1, f0_b1, f0_w2, f0_s2, f0_b2, wq, wkv, pos, scale_p, dwc_w, dwc_b, proj_w, proj_b, dw1_w, dw1_s, dw1_b, f1_w1, f1_s1, f1_b1, f1_w2, f1_s2, f1_b2):
            C = x.shape[1]
            x = x + _conv_bn(x, dw0_w, dw0_s, dw0_b, groups=C)
            x = x + _ffn(x, f0_w1, f0_s1, f0_b1, f0_w2, f0_s2, f0_b2)
            x = x + _windowed_attn(x, wq, wkv, pos, scale_p, dwc_w, dwc_b, proj_w, proj_b)
            x = x + _conv_bn(x, dw1_w, dw1_s, dw1_b, groups=C)
            x = x + _ffn(x, f1_w1, f1_s1, f1_b1, f1_w2, f1_s2, f1_b2)
            return x
        key = jax.random.key(seed)
        ks = iter(jax.random.split(key, 32))
        rn = lambda shape, s=0.02: jax.random.normal(next(ks), shape, jnp.float32) * s
        C, H, B = (64, 16, 32)
        hid, hd = (2 * C, C // NH)
        d = {'x': jax.random.normal(next(ks), (B, C, H, H), jnp.float32)}
        d.update(dw0_w=rn((C, 1, 3, 3)), dw0_s=jnp.ones(C), dw0_b=jnp.zeros(C))
        d.update(f0_w1=rn((hid, C, 1, 1)), f0_s1=jnp.ones(hid), f0_b1=jnp.zeros(hid), f0_w2=rn((C, hid, 1, 1)), f0_s2=jnp.ones(C), f0_b2=jnp.zeros(C))
        d.update(wq=rn((C, C)), wkv=rn((2 * C, C)), pos=rn((1, WR * WR, C)), scale_p=rn((1, 1, C)), dwc_w=rn((hd, 1, 5, 5)), dwc_b=jnp.zeros(hd), proj_w=rn((C, C)), proj_b=jnp.zeros(C))
        d.update(dw1_w=rn((C, 1, 3, 3)), dw1_s=jnp.ones(C), dw1_b=jnp.zeros(C))
        d.update(f1_w1=rn((hid, C, 1, 1)), f1_s1=jnp.ones(hid), f1_b1=jnp.zeros(hid), f1_w2=rn((C, hid, 1, 1)), f1_s2=jnp.ones(C), f1_b2=jnp.zeros(C))
        return d
    _L0_conv_all = _L0_conv_setup()
    _L0_conv_in = {k: v for k, v in _L0_conv_all.items() if k in ('dw0_w', 'dw0_s', 'dw0_b', 'f0_w1', 'f0_s1', 'f0_b1', 'f0_w2', 'f0_s2', 'f0_b2', 'wq', 'wkv', 'pos', 'scale_p', 'dwc_w', 'dwc_b', 'proj_w', 'proj_b', 'dw1_w', 'dw1_s', 'dw1_b', 'f1_w1', 'f1_s1', 'f1_b1', 'f1_w2', 'f1_s2', 'f1_b2')}
    del _L0_conv_all
    return {'x': x, 'L0_conv_dw0_w': _L0_conv_in['dw0_w'], 'L0_conv_dw0_s': _L0_conv_in['dw0_s'], 'L0_conv_dw0_b': _L0_conv_in['dw0_b'], 'L0_conv_f0_w1': _L0_conv_in['f0_w1'], 'L0_conv_f0_s1': _L0_conv_in['f0_s1'], 'L0_conv_f0_b1': _L0_conv_in['f0_b1'], 'L0_conv_f0_w2': _L0_conv_in['f0_w2'], 'L0_conv_f0_s2': _L0_conv_in['f0_s2'], 'L0_conv_f0_b2': _L0_conv_in['f0_b2'], 'L0_conv_wq': _L0_conv_in['wq'], 'L0_conv_wkv': _L0_conv_in['wkv'], 'L0_conv_pos': _L0_conv_in['pos'], 'L0_conv_scale_p': _L0_conv_in['scale_p'], 'L0_conv_dwc_w': _L0_conv_in['dwc_w'], 'L0_conv_dwc_b': _L0_conv_in['dwc_b'], 'L0_conv_proj_w': _L0_conv_in['proj_w'], 'L0_conv_proj_b': _L0_conv_in['proj_b'], 'L0_conv_dw1_w': _L0_conv_in['dw1_w'], 'L0_conv_dw1_s': _L0_conv_in['dw1_s'], 'L0_conv_dw1_b': _L0_conv_in['dw1_b'], 'L0_conv_f1_w1': _L0_conv_in['f1_w1'], 'L0_conv_f1_s1': _L0_conv_in['f1_s1'], 'L0_conv_f1_b1': _L0_conv_in['f1_b1'], 'L0_conv_f1_w2': _L0_conv_in['f1_w2'], 'L0_conv_f1_s2': _L0_conv_in['f1_s2'], 'L0_conv_f1_b2': _L0_conv_in['f1_b2']}

def reference(x, L0_conv_dw0_w, L0_conv_dw0_s, L0_conv_dw0_b, L0_conv_f0_w1, L0_conv_f0_s1, L0_conv_f0_b1, L0_conv_f0_w2, L0_conv_f0_s2, L0_conv_f0_b2, L0_conv_wq, L0_conv_wkv, L0_conv_pos, L0_conv_scale_p, L0_conv_dwc_w, L0_conv_dwc_b, L0_conv_proj_w, L0_conv_proj_b, L0_conv_dw1_w, L0_conv_dw1_s, L0_conv_dw1_b, L0_conv_f1_w1, L0_conv_f1_s1, L0_conv_f1_b1, L0_conv_f1_w2, L0_conv_f1_s2, L0_conv_f1_b2):
    import jax
    import jax.numpy as jnp

    def _L0_conv_ref(x, dw0_w, dw0_s, dw0_b, f0_w1, f0_s1, f0_b1, f0_w2, f0_s2, f0_b2, wq, wkv, pos, scale_p, dwc_w, dwc_b, proj_w, proj_b, dw1_w, dw1_s, dw1_b, f1_w1, f1_s1, f1_b1, f1_w2, f1_s2, f1_b2):
        import jax, jax.numpy as jnp
        from jax import lax
        import numpy as np
        WR = 7
        NH = 4
        FF = 3.0

        def _conv_bn(x, w, s, b, groups=1):
            y = lax.conv_general_dilated(x, w, (1, 1), 'SAME', dimension_numbers=('NCHW', 'OIHW', 'NCHW'), feature_group_count=groups)
            return y * s[None, :, None, None] + b[None, :, None, None]

        def _ffn(x, w1, s1, b1, w2, s2, b2):
            return _conv_bn(jax.nn.relu(_conv_bn(x, w1, s1, b1)), w2, s2, b2)

        def _focus(t):
            n0 = jnp.linalg.norm(t, axis=-1, keepdims=True)
            tp = t ** FF
            return tp / jnp.linalg.norm(tp, axis=-1, keepdims=True) * n0

        def _attn(xw, wq, wkv, pos, scale_p, dwc_w, dwc_b, proj_w, proj_b):
            Bw, N, C = xw.shape
            hd = C // NH
            q = xw @ wq.T
            kv = xw @ wkv.T
            k, v = (kv[..., :C], kv[..., C:])
            k = k + pos
            sc = jax.nn.softplus(scale_p)
            q = (jax.nn.relu(q) + 1e-06) / sc
            k = (jax.nn.relu(k) + 1e-06) / sc
            q, k = (_focus(q), _focus(k))
            heads = lambda t: t.reshape(Bw, N, NH, hd).transpose(0, 2, 1, 3).reshape(Bw * NH, N, hd)
            q, k, v = (heads(q), heads(k), heads(v))
            z = 1.0 / (jnp.einsum('bic,bc->bi', q, k.sum(axis=1)) + 1e-06)
            if N * N * (hd + hd) > hd * hd * (N + N):
                kv2 = jnp.einsum('bjc,bjd->bcd', k, v)
                y = jnp.einsum('bic,bcd,bi->bid', q, kv2, z)
            else:
                qk = jnp.einsum('bic,bjc->bij', q, k)
                y = jnp.einsum('bij,bjd,bi->bid', qk, v, z)
            num = int(round(N ** 0.5))
            fm = v.reshape(-1, num, num, hd).transpose(0, 3, 1, 2)
            fm = lax.conv_general_dilated(fm, dwc_w, (1, 1), 'SAME', dimension_numbers=('NCHW', 'OIHW', 'NCHW'), feature_group_count=hd)
            fm = fm + dwc_b[None, :, None, None]
            y = y + fm.transpose(0, 2, 3, 1).reshape(-1, N, hd)
            y = y.reshape(Bw, NH, N, hd).transpose(0, 2, 1, 3).reshape(Bw, N, C)
            return y @ proj_w.T + proj_b

        def _windowed_attn(x, wq, wkv, pos, scale_p, dwc_w, dwc_b, proj_w, proj_b):
            B, C, H, W = x.shape
            xh = x.transpose(0, 2, 3, 1)
            pb, pr = (-H % WR, -W % WR)
            xh = jnp.pad(xh, ((0, 0), (0, pb), (0, pr), (0, 0)))
            pH, pW = (H + pb, W + pr)
            nH, nW = (pH // WR, pW // WR)
            xw = xh.reshape(B, nH, WR, nW, WR, C).transpose(0, 1, 3, 2, 4, 5)
            xw = xw.reshape(B * nH * nW, WR * WR, C)
            xw = _attn(xw, wq, wkv, pos, scale_p, dwc_w, dwc_b, proj_w, proj_b)
            xh = xw.reshape(B, nH, nW, WR, WR, C).transpose(0, 1, 3, 2, 4, 5).reshape(B, pH, pW, C)
            return xh[:, :H, :W].transpose(0, 3, 1, 2)

        def _forward(x, dw0_w, dw0_s, dw0_b, f0_w1, f0_s1, f0_b1, f0_w2, f0_s2, f0_b2, wq, wkv, pos, scale_p, dwc_w, dwc_b, proj_w, proj_b, dw1_w, dw1_s, dw1_b, f1_w1, f1_s1, f1_b1, f1_w2, f1_s2, f1_b2):
            C = x.shape[1]
            x = x + _conv_bn(x, dw0_w, dw0_s, dw0_b, groups=C)
            x = x + _ffn(x, f0_w1, f0_s1, f0_b1, f0_w2, f0_s2, f0_b2)
            x = x + _windowed_attn(x, wq, wkv, pos, scale_p, dwc_w, dwc_b, proj_w, proj_b)
            x = x + _conv_bn(x, dw1_w, dw1_s, dw1_b, groups=C)
            x = x + _ffn(x, f1_w1, f1_s1, f1_b1, f1_w2, f1_s2, f1_b2)
            return x
        return _forward(x, dw0_w, dw0_s, dw0_b, f0_w1, f0_s1, f0_b1, f0_w2, f0_s2, f0_b2, wq, wkv, pos, scale_p, dwc_w, dwc_b, proj_w, proj_b, dw1_w, dw1_s, dw1_b, f1_w1, f1_s1, f1_b1, f1_w2, f1_s2, f1_b2)

    def _gn(v, G=32, eps=1e-05):
        B_, C_, H_, W_ = v.shape
        g = v.reshape(B_, G, C_ // G, H_, W_)
        m = jnp.mean(g, axis=(2, 3, 4), keepdims=True)
        s = jnp.var(g, axis=(2, 3, 4), keepdims=True)
        return ((g - m) / jnp.sqrt(s + eps)).reshape(v.shape)

    def _ln_c(v, eps=1e-06):
        m = jnp.mean(v, axis=1, keepdims=True)
        s = jnp.var(v, axis=1, keepdims=True)
        return (v - m) / jnp.sqrt(s + eps)

    def _ln_t(v, eps=1e-05):
        m = jnp.mean(v, axis=-1, keepdims=True)
        s = jnp.var(v, axis=-1, keepdims=True)
        return (v - m) / jnp.sqrt(s + eps)

    def _to_tokens(v):
        B_, C_, H_, W_ = v.shape
        return v.reshape(B_, C_, H_ * W_).transpose(0, 2, 1)

    def _from_tokens(t, like):
        B_, C_, H_, W_ = like.shape
        return t.transpose(0, 2, 1).reshape(B_, C_, H_, W_)
    x = _L0_conv_ref(x, L0_conv_dw0_w, L0_conv_dw0_s, L0_conv_dw0_b, L0_conv_f0_w1, L0_conv_f0_s1, L0_conv_f0_b1, L0_conv_f0_w2, L0_conv_f0_s2, L0_conv_f0_b2, L0_conv_wq, L0_conv_wkv, L0_conv_pos, L0_conv_scale_p, L0_conv_dwc_w, L0_conv_dwc_b, L0_conv_proj_w, L0_conv_proj_b, L0_conv_dw1_w, L0_conv_dw1_s, L0_conv_dw1_b, L0_conv_f1_w1, L0_conv_f1_s1, L0_conv_f1_b1, L0_conv_f1_w2, L0_conv_f1_s2, L0_conv_f1_b2)
    return x

_drawn_inputs = setup_inputs


def setup_inputs(seed=0):
    import zlib

    import numpy as np

    out = dict(_drawn_inputs(seed))
    spreads = {'L0_conv_dw0_s': (1.0, 0.6),
     'L0_conv_dw0_b': (0.0, 0.1),
     'L0_conv_f0_s1': (1.0, 0.6),
     'L0_conv_f0_b1': (0.0, 0.457),
     'L0_conv_f0_s2': (1.0, 0.6),
     'L0_conv_f0_b2': (0.0, 0.1),
     'L0_conv_dwc_b': (0.0, 0.535),
     'L0_conv_proj_b': (0.0, 0.1),
     'L0_conv_dw1_s': (1.0, 0.6),
     'L0_conv_dw1_b': (0.0, 0.1),
     'L0_conv_f1_s1': (1.0, 0.6),
     'L0_conv_f1_b1': (0.0, 0.531),
     'L0_conv_f1_s2': (1.0, 0.6),
     'L0_conv_f1_b2': (0.0, 0.1)}
    factors = {'L0_conv_wq': 8.0,
     'L0_conv_wkv': 6.137,
     'L0_conv_pos': 8.0,
     'L0_conv_scale_p': 8.0,
     'L0_conv_dwc_w': 8.0,
     'L0_conv_proj_w': 3.438}
    for name, (base, spread) in spreads.items():
        noise = np.random.default_rng([zlib.crc32(name.encode()), seed]).standard_normal(out[name].shape)
        drawn = base * np.exp(spread * noise) if base else spread * noise
        out[name] = jnp.asarray(drawn.astype(out[name].dtype))
    for name, factor in factors.items():
        out[name] = (out[name] * factor).astype(out[name].dtype)
    return out
```

```python
from contextlib import ExitStack

import numpy as np

import concourse.bass as bass
from concourse import mybir

F32 = mybir.dt.float32
BF16 = mybir.dt.bfloat16
ALU = mybir.AluOpType
ACT = mybir.ActivationFunctionType
AX_X = mybir.AxisListType.X

B, C, HW, HID = 32, 64, 16, 128
NH, HD, WR = 4, 16, 7
PX = HW * HW
NG = 8
GP = 2
GC = GP * PX
TOK = WR * HW
NT = 5
TC = 2 * C
PITCH = HW + 1
PROWS = 2 * HW + 1
PADDED = 3 + (PROWS + 2) * PITCH
EPS = 1e-6

CONSTS = [("ident", 128), ("mask_band", 128), ("mask_bot", 128), ("bot_sel", 64), ("head_mask", 64),
          ("win_band", 3), ("win_bot", 6), ("pos_sel", 256), ("pad_sum", 96), ("pad_of", 256), ("s1", WR * 35)]
WEIGHTS = [("dw0w", 9), ("dw0s", 1), ("dw0b", 1), ("dw1w", 9), ("dw1s", 1), ("dw1b", 1),
           ("f0b1", 1), ("f0s1", 1), ("f0b2", 1), ("f0s2", 1), ("f1b1", 1), ("f1s1", 1), ("f1b2", 1), ("f1s2", 1),
           ("scale", 1), ("dwcb", 1), ("projb", 1), ("dwcw", 16), ("pos", 64),
           ("w1_0", 128), ("w1_1", 128), ("w2_0", 128), ("w2_1", 128), ("wqk", 128), ("wv", 128), ("proj", 128)]


def columns(table):
    at, out = 0, {}
    for name, n in table:
        out[name] = (at, at + n)
        at += n
    return out, at


CCOL, CTOT = columns(CONSTS)
WCOL, WTOT = columns(WEIGHTS)


def shape_constants():
    c = np.zeros((128, CTOT), np.float32)

    def put(name):
        a, b = CCOL[name]
        return c[:, a:b]

    put("ident")[:] = np.eye(128)
    tok = np.arange(128)
    band_ok = tok < TOK
    wx = np.minimum(tok % HW // WR, 2)
    n_band = tok // HW * WR + tok % HW - WR * wx
    pair, low = tok // 64, tok % 64
    bot_ok = low >= 32
    n_bot = (low // HW - 2) * WR + tok % HW - WR * wx
    same = wx[:, None] == wx[None]
    put("mask_band")[:] = same & band_ok[:, None] & band_ok[None]
    put("mask_bot")[:] = same & bot_ok[:, None] & bot_ok[None] & (pair[:, None] == pair[None])
    real = np.flatnonzero(bot_ok)
    put("bot_sel")[real, np.arange(64)] = 1
    put("head_mask")[:] = (tok[:, None] % C // HD) == (np.arange(C)[None] % NH)
    put("win_band")[:] = (wx[:, None] == np.arange(3)[None]) & band_ok[:, None]
    for j in range(2):
        put("win_bot")[:, 3 * j:3 * j + 3] = (wx[:, None] == np.arange(3)[None]) & (bot_ok & (pair == j))[:, None]
    for k, (n_of, ok) in enumerate([(n_band, band_ok), (n_bot, bot_ok)]):
        for p in np.flatnonzero(ok):
            put("pos_sel")[n_of[p], 128 * k + p] = 1
    n = np.arange(WR * WR)
    right, below = n % WR >= 2, n // WR >= 2
    for part in (0, 32, 64):
        for kind, padding in enumerate([right, below, right | below]):
            put("pad_sum")[0:WR * WR, part + kind] = padding
        put("pad_of")[part, 0:128] = band_ok & (wx == 2)
        put("pad_of")[part + 1, 128:256] = bot_ok & (wx < 2)
        put("pad_of")[part + 2, 128:256] = bot_ok & (wx == 2)
    s1 = put("s1").reshape(128, WR, 35)
    for dy in range(5):
        for dx in range(5):
            for y_out in range(WR):
                y_in = y_out + dy - 2
                if 0 <= y_in < WR:
                    s1[dy * 5 + dx, y_out, y_in * 5 + dx] = 1
    s2 = np.zeros((35, HW, TOK), np.float32)
    for y in range(WR):
        for dx in range(5):
            for x_out in range(HW):
                x_in = x_out + dx - 2
                if 0 <= x_in < HW and min(x_in // WR, 2) == min(x_out // WR, 2):
                    s2[y * 5 + dx, x_out, y * HW + x_in] = 1
    return c, s2.reshape(35, HW * TOK)


class Count:

    def __init__(self, sem):
        self.sem, self.n = sem, 0

    def mark(self, ins):
        ins.then_inc(self.sem, 1)
        self.n += 1
        return self.n


def window_block_kernel(nc, x, weights, consts, s2_in, out):
    PE_TAPS = [[0, 2], [0, 2, 6]]
    TAPS = [[t for t in range(9) if t not in PE_TAPS[s]] for s in range(2)]

    x_v = x.rearrange("(g j a) c h w -> g (a c) j (h w)", j=GP, a=2)
    out_v = out.rearrange("(g j a) c h w -> g (a c) j (h w)", j=GP, a=2)

    with ExitStack() as ctx:
        def sb(name, *shape, dt=F32):
            return ctx.enter_context(nc.sbuf_tensor(name, list(shape), dt))

        def sem(name):
            return ctx.enter_context(nc.semaphore(name))

        ps = ctx.enter_context(nc.psum_tensor("ps", [128, 8 * 512], F32))

        def bank(k, n=1):
            return ps[:, 512 * k:512 * (k + n)]

        P_DW, P_H, P_QK, P_V = 0, 1, 3, 6

        cst = sb("cst", 128, CTOT)
        wts = sb("wts", 128, WTOT)

        def cc(name, p=128):
            a, b = CCOL[name]
            return cst[0:p, a:b]

        def ww(name, p=128):
            a, b = WCOL[name]
            return wts[0:p, a:b]

        ident = cc("ident")

        xin = sb("xin", 128, NG, GC)
        xp = sb("xp", 128, 2, PADDED)
        acc = sb("acc", 128, 2, PROWS * HW)
        x1 = sb("x1", 128, 2, GC)
        hid = sb("hid", 128, 2, 2, GC)
        x2 = sb("x2", 128, NG, GC)
        dwf = sb("dwf", 128, 2, 9)
        diag = sb("diag", 128, 5, 128)
        w1s = sb("w1s", 128, 2, 128)
        w2s = sb("w2s", 64, 2, 128)
        w1t = sb("w1t", 128, 2, 2, 128)
        w2t = sb("w2t", 128, 2, C)
        wqks = sb("wqks", 128, 128)
        wqk = sb("wqk_bd", 128, 4, C)
        wv = sb("wv_bd", 128, 2, C)
        projt = sb("projt", 128, 2, C)
        projc = sb("projc", 128, 1)
        sp = sb("sp", 128, 12)
        inv = sb("inv", 128, 1)
        dinv = sb("dinv", 64, 64)
        ones = sb("ones", 64, 128)
        bc = sb("bc", 128, C)
        etile = sb("etile", 128, 2, C)
        pose = sb("pose", 128, NT, 2, C)
        kpad = sb("kpad", 49, 6, C)
        kpn = sb("kpn", 49, 4)
        padr = sb("padr", 96, C)
        padrhs = sb("padrhs", 96, 8, C, dt=BF16)
        pad_of = sb("pad_of", 96, 2, 128, dt=BF16)
        tqk = sb("tqk", 128, 2, NT, 2 * TC)
        kraw = sb("kraw", 128, NT, TC)
        sq = sb("sq", 128, NT, 2 * TC)
        t3 = sb("t3", 128, 2, NT, 2 * TC)
        s6 = sb("s6", 128, NT, 2 * TC)
        nrm = sb("nrm", 128, 4, 20)
        foc = sb("foc", 128, 2, 20)
        kf = sb("kf", 128, NT, TC)
        vband = sb("vband", 128, NG, 8, C)
        vbot = sb("vbot", 128, NG, 2, C)
        vmb = sb("vmb", 128, 3, 8, C)
        vmt = sb("vmt", 128, 6, 2, C)
        kv = sb("kv", 128, 18, C)
        prod = sb("prod", 128, NT, TC)
        den = sb("den", 128, 5, 40)
        q2 = sb("q2", 128, NT, TC)
        qt = sb("qt", 128, GP, PX)
        y = sb("y", 128, NG, GC)
        rrow = sb("rrow", 35, WR, HD)
        tband = sb("tband", TOK, HD, TOK)
        tbot = sb("tbot", 128, HD, 64)
        fmband = sb("fmband", TOK, NG * 8, C)
        fmbot = sb("fmbot", 64, NG * 2, C)
        s2 = fmband[0:35, 0:HW * TOK // C, :].rearrange("p s c -> p (s c)")

        w_in, c_in, s2_arrived = sem("w_in"), sem("c_in"), sem("s2_arrived")
        x_in = [sem(f"x_in{g}") for g in range(NG)]
        zeroed = sem("zeroed")
        xp_ready, dw_ps, x1_ready = sem("xp_ready"), sem("dw_ps"), sem("x1_ready")
        h_ps, h_ready, f_ps, res_ready = sem("h_ps"), sem("h_ready"), sem("f_ps"), sem("res_ready")
        qk_ps, v_ps, tq_ready, kraw_ready, tk_ready = sem("qk_ps"), sem("v_ps"), sem("tq_ready"), sem("kraw_ready"), sem("tk_ready")
        krelu_ready = sem("krelu_ready")
        sq_ready, t3_ready, s6_ready = sem("sq_ready"), sem("t3_ready"), sem("s6_ready")
        ratio_ready, foc_ready, kf_ready = sem("ratio_ready"), sem("foc_ready"), sem("kf_ready")
        v_ready, vm_ready = sem("v_ready"), sem("vm_ready")
        kv_ps, kv_ready, ks_ps, prod_ready, q2_ready = sem("kv_ps"), sem("kv_ready"), sem("ks_ps"), sem("prod_ready"), sem("q2_ready")
        qt_ps, qt_ready, y_ps, y_ready = sem("qt_ps"), sem("qt_ready"), sem("y_ps"), sem("y_ready")
        fm_ps, fm_ready = sem("fm_ps"), sem("fm_ready")
        tp_ps, ysum_ready, pj_ps = sem("tp_ps"), sem("ysum_ready"), sem("pj_ps")
        stored = sem("stored")
        exp_ready, ln_ready, pad_root, band_matrix = sem("exp_ready"), sem("ln_ready"), sem("pad_root"), sem("band_matrix")
        ffn_ps, vp_ps, spread_ps, projc_ps, inv_ps = sem("ffn_ps"), sem("vp_ps"), sem("spread_ps"), sem("projc_ps"), sem("inv_ps")
        pos_ps, pads_ps, matrix_ps = sem("pos_ps"), sem("pads_ps"), sem("matrix_ps")
        abs_ready, u_ready, scaled, diag_ready, blocks = sem("abs_ready"), sem("u_ready"), sem("scaled"), sem("diag_ready"), sem("blocks")
        inv_ready, pos_ready, spread_ready, e_ready = sem("inv_ready"), sem("pos_ready"), sem("spread_ready"), sem("e_ready")
        pad_ratio, pads_focused, set_up, bottom_matrix = sem("pad_ratio"), sem("pads_focused"), sem("set_up"), sem("bottom_matrix")
        dve_step = sem("dve_step")

        FM_SLOTS = {5: [0], 6: [1, 2], 7: [3, 4], 9: [5], 10: [6, 7], 11: [8, 9]}
        FM_BANK = [1, 1, 2, 1, 2, 2, 3, 4, 4, 6]
        MIXED = NG + 4
        SLOTS = 2 * NG

        def dw_bank(m):
            return bank(7 if m >= MIXED and m % 2 == 0 else P_DW)

        def turn_bank(g):
            return bank(1 if g < 4 else 3 + g % 2)

        def project_bank(g):
            return bank(2 if g < 4 else 5 + g % 2)

        block = ctx.enter_context(nc.Block())

        def padded(m):
            v = xp[:, m % 2, 1 + PITCH:1 + PITCH + GP * (HW + 1) * PITCH]
            return v.rearrange("p (j h w) -> p j h w", j=GP, w=PITCH)[:, :, 0:HW, 0:HW]

        def tap_rows(m, tap):
            dy, dx = tap // 3 - 1, tap % 3 - 1
            at = 1 + (1 + dy) * PITCH + dx
            return xp[:, m % 2, at:at + PROWS * PITCH].rearrange("p (r w) -> p r w", w=PITCH)[:, :, 0:HW]

        def shifted(m, tap):
            dy, dx = tap // 3 - 1, tap % 3 - 1
            at = 1 + (1 + dy) * PITCH + dx
            full = xp[:, m % 2, :]
            return bass.AP(full.tensor, full.offset + at, [list(full.ap[0]), [(HW + 1) * PITCH, GP], [PITCH, HW], [1, HW]])

        @block.sync
        def _(eng):
            eng.dma_start(wts[:, :], weights).then_inc(w_in, 16)
            for g in range(NG):
                eng.dma_start(xin[:, g, :].rearrange("p (j n) -> p j n", j=GP), x_v[g]).then_inc(x_in[g], 16)
            for g in range(NG):
                eng.wait_ge(res_ready, NG + g + 1)
                eng.dma_start(out_v[g], xin[:, g, :].rearrange("p (j n) -> p j n", j=GP)).then_inc(stored, 16)
            eng.wait_ge(stored, 16 * NG)

        @block.gpsimd
        def _(eng):
            eng.memset(xp[:, :, :], 0.0).then_inc(zeroed, 1)
            eng.memset(w1t[:, :, :, :], 0.0).then_inc(zeroed, 1)
            eng.memset(wqk[:, :, :], 0.0).then_inc(zeroed, 1)
            eng.memset(wv[:, :, :], 0.0).then_inc(zeroed, 1)
            eng.memset(projt[:, :, :], 0.0).then_inc(zeroed, 1)
            eng.memset(ones[:, :], 1.0).then_inc(zeroed, 1)
            eng.memset(tbot[:, :, :], 0.0).then_inc(zeroed, 1)
            eng.wait_ge(c_in, 16)
            eng.wait_ge(e_ready, 1)
            for g in range(NG):
                eng.wait_ge(krelu_ready, g + 1)
                if g >= 2:
                    eng.wait_ge(t3_ready, g - 1)
                    eng.wait_ge(sq_ready, g - 1)
                eng.tensor_tensor(tqk[:, g % 2, :, TC:2 * TC].rearrange("p t (a c) -> p t a c", a=2),
                                  kraw[:, :, :].rearrange("p t (a c) -> p t a c", a=2),
                                  etile[:, :, :].unsqueeze(1).broadcast_to([128, NT, 2, C]), ALU.add).then_inc(tk_ready, 1)
                eng.wait_ge(sq_ready, g + 1)
                eng.wait_ge(tk_ready, g + 1)
                if g >= 2:
                    eng.wait_ge(q2_ready, g - 1)
                eng.tensor_tensor(t3[:, g % 2, :, :], sq[:, :, :], tqk[:, g % 2, :, :], ALU.mult).then_inc(t3_ready, 1)
                eng.wait_ge(v_ready, 2 * (g + 1))
                if g >= 1:
                    eng.wait_ge(kv_ps, g)
                for w in range(3):
                    eng.tensor_scalar(vmb[:, w, :, :], vband[:, g, :, :], cc("win_band")[:, w:w + 1], 0.0,
                                      ALU.mult, ALU.add)
                for w in range(6):
                    last = eng.tensor_scalar(vmt[:, w, :, :], vbot[:, g, :, :], cc("win_bot")[:, w:w + 1], 0.0,
                                             ALU.mult, ALU.add)
                last.then_inc(vm_ready, 1)

        @block.scalar
        def _(eng):
            eng.dma_start(cst[:, :], consts).then_inc(c_in, 16)
            eng.dma_start(s2[:, :], s2_in).then_inc(s2_arrived, 16)
            def pad(g):
                eng.wait_ge(x_in[g], 16)
                if g == 0:
                    eng.wait_ge(zeroed, 1)
                if g >= 2:
                    eng.wait_ge(x1_ready, g - 1)
                    eng.wait_ge(dw_ps, g - 1)
                eng.activation(padded(g), xin[:, g, :].rearrange("p (j h w) -> p j h w", j=GP, h=HW),
                               ACT.Copy).then_inc(xp_ready, 1)

            def hidden(m):
                s = m // NG
                for a in range(2):
                    eng.wait_ge(h_ps, 2 * m + a + 1)
                    if m >= 2 and a == 0:
                        eng.wait_ge(f_ps, m - 1)
                    eng.activation(hid[:, m % 2, a, :], bank(P_H + a), ACT.Relu,
                                   bias=ww(f"f{s}b1")).then_inc(h_ready, 1)

            def take_v(g):
                eng.wait_ge(v_ps, g + 1)
                eng.activation(vband[:, g, :, :], ps[:, 512 * P_V:512 * P_V + 512].rearrange("p (s c) -> p s c", c=C),
                               ACT.Copy).then_inc(v_ready, 1)
                eng.activation(vbot[:, g, :, :], ps[:, 512 * P_V + 512:512 * P_V + 640].rearrange("p (s c) -> p s c", c=C),
                               ACT.Copy).then_inc(v_ready, 1)

            def relu_k(g):
                eng.wait_ge(kraw_ready, g + 1)
                eng.activation(kraw[:, :, :], kraw[:, :, :], ACT.Relu).then_inc(krelu_ready, 1)

            def squares(g):
                eng.wait_ge(tq_ready, g + 1)
                eng.wait_ge(tk_ready, g + 1)
                if g >= 1:
                    eng.wait_ge(t3_ready, g)
                    eng.wait_ge(ratio_ready, g)
                eng.activation(sq[:, :, :], tqk[:, g % 2, :, :], ACT.Square).then_inc(sq_ready, 1)

            def sixth(g):
                eng.wait_ge(t3_ready, g + 1)
                eng.activation(s6[:, :, :], t3[:, g % 2, :, :], ACT.Square).then_inc(s6_ready, 1)

            def ratio(g):
                eng.wait_ge(ratio_ready, g + 1)
                eng.activation(foc[:, g % 2, :], nrm[:, 3, :], ACT.Sqrt).then_inc(foc_ready, 1)

            def take_qt(g):
                eng.wait_ge(qt_ps, g + 1)
                eng.activation(qt[:, :, :], bank(P_V).rearrange("p (j n) -> p j n", j=GP), ACT.Copy).then_inc(qt_ready, 1)

            def take_y(g):
                eng.wait_ge(y_ps, g + 1)
                eng.activation(y[:, g, :], bank(P_V + 1), ACT.Copy).then_inc(y_ready, 1)

            def take_fm(c):
                eng.wait_ge(fm_ps, c + 1)
                half, part = divmod(c, 5)
                if part < 4:
                    src = bank(FM_BANK[c])[0:TOK].rearrange("p (d s h) -> p s d h", d=4, h=NH)
                    dst = fmband[:, 32 * half:32 * half + 32, 16 * part:16 * part + 16]
                else:
                    src = bank(FM_BANK[c])[0:64].rearrange("p (d s h) -> p s d h", d=HD, h=NH)
                    dst = fmbot[:, 8 * half:8 * half + 8, :]
                eng.activation(dst.rearrange("p s (d h) -> p s d h", h=NH), src, ACT.Copy).then_inc(fm_ready, 1)

            pad(0)
            eng.wait_ge(abs_ready, 1)
            eng.activation(sp[:, 1:2], sp[:, 0:1], ACT.Exp, scale=-1.0).then_inc(exp_ready, 1)
            eng.wait_ge(u_ready, 1)
            eng.activation(sp[:, 3:4], sp[:, 2:3], ACT.Ln).then_inc(ln_ready, 1)
            eng.wait_ge(pad_ratio, 1)
            eng.activation(kpn[:, 2:3], kpn[:, 3:4], ACT.Sqrt).then_inc(pad_root, 1)
            for n in range(SLOTS):
                g1, g2, g3 = n - 1, n - 2, n - 3
                if 0 <= g3 < NG:
                    take_y(g3)
                if 0 <= g1 < NG:
                    take_v(g1)
                    relu_k(g1)
                if n + 1 < NG:
                    pad(n + 1)
                if 0 <= g1 < NG:
                    squares(g1)
                hidden(n)
                if 0 <= g1 < NG:
                    sixth(g1)
                for c in FM_SLOTS.get(n, []):
                    take_fm(c)
                if 0 <= g2 < NG:
                    take_qt(g2)
                if 0 <= g1 < NG:
                    ratio(g1)
                if n == 0:
                    eng.wait_ge(matrix_ps, 1)
                    for q in range(4):
                        src = bank(3 + q)[0:TOK, 0:448].rearrange("p (x y d) -> p d y x", x=4, y=WR)
                        dst = tband[:, :, :].rearrange("p d (y x) -> p d y x", x=HW)[:, :, :, 4 * q:4 * q + 4]
                        last = eng.activation(dst, src, ACT.Copy)
                    last.then_inc(band_matrix, 1)

        @block.tensor
        def _(eng):
            def conv(m):
                s, g = divmod(m, NG)
                eng.wait_ge(xp_ready, m + 1)
                if m == MIXED:
                    eng.wait_ge(y_ready, NG)
                elif m > MIXED:
                    eng.wait_ge(res_ready, m - 1)
                elif m >= 1:
                    eng.wait_ge(res_ready, m)
                taps = PE_TAPS[s]
                for i, tap in enumerate(taps):
                    last = eng.matmul(dw_bank(m), diag[:, 2 * s + i, :], shifted(m, tap), start=(i == 0), stop=(i == len(taps) - 1))
                last.then_inc(dw_ps, 1)

            def ffn1(m):
                s = m // NG
                eng.wait_ge(x1_ready, m + 1)
                if m >= 1:
                    eng.wait_ge(h_ready, 2 * m)
                eng.wait_ge(fm_ready, sum(len(v) for k, v in FM_SLOTS.items() if k < m)) if m > 5 else None
                for a in range(2):
                    eng.matmul(bank(P_H + a), w1t[:, s, a, :], x1[:, m % 2, :], start=True, stop=True).then_inc(h_ps, 1)

            def ffn2(m):
                s = m // NG
                for a in range(2):
                    eng.wait_ge(h_ready, 2 * m + a + 1)
                    last = eng.matmul(dw_bank(m)[64 * a:64 * a + 64], w2t[:, s, :], hid[:, m % 2, a, :], start=True, stop=True)
                last.then_inc(f_ps, 1)

            def by_token(g, o, w, n):
                for t in range(4):
                    at = PX * (t % 2) + TOK * (t // 2)
                    eng.matmul(ps[:, o + n * t:o + n * t + n], x2[:, g, at:at + 128], w, start=True, stop=True)
                for j in range(GP):
                    at = PX * j + PX - 64
                    last = eng.matmul(ps[64 * j:64 * j + 64, o + 4 * n:o + 5 * n], x2[:, g, at:at + 64], w,
                                      start=True, stop=True)
                return last

            def project_qk(g):
                eng.wait_ge(res_ready, g + 1)
                if g >= 2:
                    eng.wait_ge(kv_ready, g - 1)
                by_token(g, 512 * P_QK, wqk[:, :, :].rearrange("p s c -> p (s c)"), 2 * TC).then_inc(qk_ps, 1)

            def project_v(g):
                if g >= 2:
                    eng.wait_ge(y_ready, g - 1)
                    eng.wait_ge(qt_ready, g - 1)
                by_token(g, 512 * P_V, wv[:, :, :].rearrange("p s c -> p (s c)"), TC).then_inc(v_ps, 1)

            def key_value(g):
                eng.wait_ge(kf_ready, g + 1)
                eng.wait_ge(vm_ready, g + 1)
                if g + 1 < NG:
                    eng.wait_ge(kraw_ready, g + 2)
                    eng.wait_ge(tq_ready, g + 2)
                for t in range(4):
                    b, j = divmod(t, 2)
                    for a in range(2):
                        o = 512 * (P_QK + j) + 192 * b
                        eng.matmul(ps[64 * a:64 * a + 64, o:o + 192], kf[:, t, 64 * a:64 * a + 64],
                                   vmb[:, :, 2 * t + a, :], start=True, stop=True)
                for a in range(2):
                    o = 512 * (P_QK + 2)
                    last = eng.matmul(ps[64 * a:64 * a + 64, o:o + 384], kf[:, 4, 64 * a:64 * a + 64],
                                      vmt[:, :, a, :], start=True, stop=True)
                last.then_inc(kv_ps, 1)

            def key_sum(g):
                eng.wait_ge(v_ready, 2 * min(g + 2, NG))
                if g >= 1:
                    eng.wait_ge(qt_ready, g)
                    eng.wait_ge(y_ready, g)
                o = 512 * P_V
                eng.matmul(ps[:, o:o + 512], cc("mask_band"), kf[:, 0:4, :].rearrange("p t c -> p (t c)"), start=True, stop=False)
                eng.matmul(ps[:, o:o + 512], pad_of[:, 0, :], padrhs[:, :, :].rearrange("p s c -> p (s c)"),
                           start=False, stop=True)
                eng.matmul(ps[:, o + 512:o + 640], cc("mask_bot"), kf[:, 4, :], start=True, stop=False)
                eng.matmul(ps[:, o + 512:o + 640], pad_of[:, 1, :],
                           padrhs[:, 0:2, :].rearrange("p s c -> p (s c)"), start=False, stop=True).then_inc(ks_ps, 1)

            def turn_q(g):
                eng.wait_ge(q2_ready, g + 1)
                v = bank(P_V).rearrange("p (j n) -> p j n", j=GP)
                for t in range(4):
                    b, j = divmod(t, 2)
                    eng.transpose(v[:, j, TOK * b:TOK * b + TOK], q2[0:TOK, t, :], cc("ident", TOK)[:, 0:TOK])
                eng.matmul(v[:, :, PX - 32:PX], q2[:, 4, :], cc("bot_sel"), start=True, stop=True).then_inc(qt_ps, 1)

            def attend(g):
                eng.wait_ge(kv_ready, g + 1)
                eng.wait_ge(qt_ready, g + 1)
                for j in range(GP):
                    for wy in range(3):
                        for wx in range(3):
                            slot = 8 * 0 + (6 * j + 3 * wy + wx if wy < 2 else 12 + 3 * j + wx)
                            ry, rx = slice(WR * wy, min(WR * wy + WR, HW)), slice(WR * wx, min(WR * wx + WR, HW))
                            for a in range(2):
                                p = slice(64 * a, 64 * a + 64)
                                src = qt[p, j, :].rearrange("p (h w) -> p h w", w=HW)[:, ry, rx]
                                dst = ps[p, 512 * (P_V + 1) + PX * j:512 * (P_V + 1) + PX * j + PX]
                                dst = dst.rearrange("p (h w) -> p h w", w=HW)[:, ry, rx]
                                last = eng.matmul(dst, kv[p, slot, :], src, start=True, stop=True)
                last.then_inc(y_ps, 1)

            def window_conv(c):
                half, part = divmod(c, 5)
                if c == 0:
                    eng.wait_ge(bottom_matrix, 1)
                if FM_BANK[c] == 3:
                    eng.wait_ge(kv_ready, NG)
                if c == 8:
                    eng.wait_ge(fm_ready, 8)
                if c == 9:
                    eng.wait_ge(qt_ready, NG)
                eng.wait_ge(v_ready, 8 * (half + 1))
                gs = slice(4 * half, 4 * half + 4)
                out_ps = bank(FM_BANK[c])
                if part < 4:
                    for d in range(4):
                        dc = 4 * part + d
                        last = eng.matmul(out_ps[0:TOK, 128 * d:128 * d + 128], tband[:, dc, :],
                                          vband[0:TOK, gs, :, NH * dc:NH * dc + NH].rearrange("p g s h -> p (g s) h"),
                                          start=True, stop=True)
                else:
                    for dc in range(HD):
                        last = eng.matmul(out_ps[0:64, 32 * dc:32 * dc + 32], tbot[:, dc, :],
                                          vbot[:, gs, :, NH * dc:NH * dc + NH].rearrange("p g s h -> p (g s) h"),
                                          start=True, stop=True)
                last.then_inc(fm_ps, 1)

            def turn_fm(g):
                eng.wait_ge(fm_ready, 5 if g < 4 else 10)
                if g >= 6:
                    eng.wait_ge(ysum_ready, g - 1)
                v = turn_bank(g).rearrange("p (j n) -> p j n", j=GP)
                for t in range(4):
                    b, j = divmod(t, 2)
                    s = 8 * g + 2 * t
                    eng.transpose(v[:, j, TOK * b:TOK * b + TOK], fmband[:, s:s + 2, :].rearrange("p s c -> p (s c)"),
                                  cc("ident", TOK)[:, 0:TOK])
                eng.transpose(v[:, :, PX - 32:PX], fmbot[:, 2 * g:2 * g + 2, :].rearrange("p s c -> p (s c)"),
                              cc("ident", 64)[:, 0:64]).then_inc(tp_ps, 1)

            def project(g):
                eng.wait_ge(ysum_ready, g + 1)
                if FM_SLOTS.get(g + NG - 1):
                    eng.wait_ge(fm_ready, sum(len(v) for k, v in FM_SLOTS.items() if k <= g + NG - 1))
                if g >= 6:
                    eng.wait_ge(xp_ready, NG + g - 1)
                eng.matmul(project_bank(g), projt[:, :, :].rearrange("p a c -> p (a c)"), y[:, g, :],
                           start=True, stop=True).then_inc(pj_ps, 1)

            eng.wait_ge(c_in, 16)
            eng.wait_ge(diag_ready, 1)
            conv(0)
            eng.wait_ge(scaled, 1)
            for s in range(2):
                eng.transpose(bank(3)[:, 128 * s:128 * s + 128], w1s[:, s, :], ident)
            for s in range(2):
                last = eng.transpose(bank(3)[:, 256 + 64 * s:320 + 64 * s], w2s[:, s, :], cc("ident", 64)[:, 0:64])
            last.then_inc(ffn_ps, 1)
            eng.transpose(bank(4)[:, 0:64], ww("wv", 64), cc("ident", 64)[:, 0:64])
            eng.transpose(bank(4)[:, 64:128], ww("proj", 64), cc("ident", 64)[:, 0:64]).then_inc(vp_ps, 1)
            for y_out in range(WR):
                last = eng.matmul(bank(7)[0:35, HD * y_out:HD * y_out + HD],
                                  cc("s1", 25)[:, 35 * y_out:35 * y_out + 35], ww("dwcw", 25), start=True, stop=True)
            last.then_inc(spread_ps, 1)
            eng.wait_ge(inv_ready, 1)
            eng.wait_ge(zeroed, 6)
            eng.transpose(bank(5)[:, 0:128], wqks[:, :], ident)
            eng.matmul(bank(5)[:, 128:192], ones[:, :], dinv[:, :], start=True, stop=True).then_inc(inv_ps, 1)
            eng.wait_ge(blocks, 1)
            eng.matmul(bank(6)[:, 0:1], projt[:, :, :].rearrange("p a c -> p (a c)"), ww("dwcb"),
                       start=True, stop=True).then_inc(projc_ps, 1)
            ffn1(0)
            eng.wait_ge(pos_ready, 1)
            for k in range(2):
                last = eng.matmul(bank(5)[:, 256 + 64 * k:320 + 64 * k], cc("pos_sel", 49)[:, 128 * k:128 * k + 128],
                                  kpad[:, 0, :], start=True, stop=True)
            last.then_inc(pos_ps, 1)
            ffn2(0)
            eng.wait_ge(pads_focused, 1)
            eng.matmul(bank(7)[0:96, 384:448], cc("pad_sum", 49), kpad[:, 5, :], start=True, stop=True).then_inc(pads_ps, 1)
            eng.wait_ge(s2_arrived, 16)
            eng.wait_ge(set_up, 1)
            for x_out in range(HW):
                o = 112 * (x_out % 4)
                last = eng.matmul(bank(3 + x_out // 4)[0:TOK, o:o + 112], s2[:, TOK * x_out:TOK * x_out + TOK],
                                  rrow[:, :, :].rearrange("p y d -> p (y d)"), start=True, stop=True)
            last.then_inc(matrix_ps, 1)
            for n in range(1, SLOTS):
                g1, g2, g3, c = n - 1, n - 2, n - 3, n + 1 - NG
                if n == 1:
                    eng.wait_ge(band_matrix, 1)
                if 0 <= g1 < NG:
                    project_qk(g1)
                if 0 <= g3 < NG:
                    attend(g3)
                if n >= MIXED and c < NG:
                    turn_fm(c)
                conv(n)
                if 0 <= g1 < NG:
                    project_v(g1)
                if 0 <= g2 < NG:
                    key_value(g2)
                    key_sum(g2)
                if n >= MIXED and c < NG:
                    project(c)
                ffn1(n)
                ffn2(n)
                for k in FM_SLOTS.get(n, []):
                    window_conv(k)
                if n < MIXED and 0 <= c:
                    turn_fm(c)
                if 0 <= g2 < NG:
                    turn_q(g2)
                if n < MIXED and 0 <= c:
                    project(c)

        @block.vector
        def _(eng):
            step = Count(dve_step)

            def link(ins):
                eng.wait_ge(dve_step, step.mark(ins))

            def fold(s):
                link(eng.tensor_scalar(dwf[:, s, :], ww(f"dw{s}w"), ww(f"dw{s}s"), None, ALU.mult))
                link(eng.tensor_scalar(dwf[:, s, 4:5], dwf[:, s, 4:5], 1.0, None, ALU.add))

            def diagonals(s):
                for i, tap in enumerate(PE_TAPS[s]):
                    last = eng.tensor_scalar(diag[:, 2 * s + i, :], ident, dwf[:, s, tap:tap + 1], None, ALU.mult)
                return last

            def tap(m, i):
                s = m // NG
                k = TAPS[s][i]
                a = acc[:, m % 2, :].rearrange("p (r w) -> p r w", w=HW)
                w = dwf[:, s, k:k + 1]
                if i == 0:
                    eng.wait_ge(xp_ready, m + 1)
                    step.mark(eng.tensor_scalar(a, tap_rows(m, k), w, ww(f"dw{s}b"), ALU.mult, ALU.add))
                else:
                    eng.wait_ge(dve_step, step.last)
                    step.mark(eng.scalar_tensor_tensor(a, tap_rows(m, k), w, a, ALU.mult, ALU.add))
                step.last = step.n

            def combine(m):
                eng.wait_ge(dw_ps, m + 1)
                eng.wait_ge(dve_step, step.last)
                if m >= 2:
                    eng.wait_ge(h_ps, 2 * (m - 1))
                full = acc[:, m % 2, :]
                a = bass.AP(full.tensor, full.offset, [list(full.ap[0]), [(HW + 1) * HW, GP], [1, PX]])
                eng.tensor_tensor(x1[:, m % 2, :].rearrange("p (j n) -> p j n", j=GP),
                                  dw_bank(m).rearrange("p (j n) -> p j n", j=GP), a, ALU.add).then_inc(x1_ready, 1)

            def residual(m):
                s, g = divmod(m, NG)
                eng.wait_ge(f_ps, m + 1)
                eng.wait_ge(x1_ready, m + 1)
                dst = x2[:, g, :] if s == 0 else xin[:, g, :]
                eng.scalar_tensor_tensor(dst, dw_bank(m), ww(f"f{s}b2"), x1[:, m % 2, :], ALU.add, ALU.add)\
                   .then_inc(res_ready, 1)

            def q_t(g):
                eng.wait_ge(qk_ps, g + 1)
                if g >= 2:
                    eng.wait_ge(t3_ready, g - 1)
                src = ps[:, 512 * P_QK:512 * P_QK + 1280].rearrange("p (t n) -> p t n", t=NT)
                e = etile[:, :, :].rearrange("p a c -> p (a c)").unsqueeze(1).broadcast_to([128, NT, TC])
                eng.scalar_tensor_tensor(tqk[:, g % 2, :, 0:TC], src[:, :, 0:TC], 0.0, e, ALU.max, ALU.add)\
                   .then_inc(tq_ready, 1)

            def k_raw(g):
                eng.wait_ge(qk_ps, g + 1)
                if g >= 1:
                    eng.wait_ge(tk_ready, g)
                src = ps[:, 512 * P_QK:512 * P_QK + 1280].rearrange("p (t n) -> p t n", t=NT)
                eng.tensor_tensor(kraw[:, :, :], src[:, :, TC:2 * TC], pose[:, :, :, :].rearrange("p t a c -> p t (a c)"),
                                  ALU.add).then_inc(kraw_ready, 1)

            def norm2(g):
                eng.wait_ge(sq_ready, g + 1)
                step.mark(eng.tensor_reduce(nrm[:, 0, :], sq[:, :, :].rearrange("p t (s c) -> p (t s) c", c=C), AX_X, ALU.add))

            def norm6(g):
                eng.wait_ge(s6_ready, g + 1)
                link(eng.tensor_reduce(nrm[:, 1, :], s6[:, :, :].rearrange("p t (s c) -> p (t s) c", c=C), AX_X, ALU.add))
                link(eng.reciprocal(nrm[:, 2, :], nrm[:, 1, :]))
                eng.tensor_tensor(nrm[:, 3, :], nrm[:, 0, :], nrm[:, 2, :], ALU.mult).then_inc(ratio_ready, 1)

            def ratio_of(g, qk, n):
                f = foc[:, g % 2, :].rearrange("p (t s a) -> p t s a", s=2, a=2)[:, :, qk, :]
                return f.unsqueeze(3).broadcast_to([128, NT, 2, n])

            def k_focus(g):
                eng.wait_ge(foc_ready, g + 1)
                if g >= 1:
                    eng.wait_ge(ks_ps, g)
                eng.tensor_tensor(kf[:, :, :].rearrange("p t (a c) -> p t a c", a=2),
                                  t3[:, g % 2, :, TC:2 * TC].rearrange("p t (a c) -> p t a c", a=2),
                                  ratio_of(g, 1, C), ALU.mult).then_inc(kf_ready, 1)

            def take_kv(g):
                eng.wait_ge(kv_ps, g + 1)
                if g >= 1:
                    eng.wait_ge(y_ps, g)
                src = ps[:, 512 * P_QK:512 * P_QK + 1536].rearrange("p (k n) -> p k n", k=3)[:, :, 0:384]
                mask = cc("head_mask").unsqueeze(1).unsqueeze(1).broadcast_to([128, 3, 6, C])
                eng.tensor_tensor(kv[:, :, :].rearrange("p (k s) c -> p k s c", k=3),
                                  src.rearrange("p k (s c) -> p k s c", c=C), mask, ALU.mult).then_inc(kv_ready, 1)

            def q_scale(g):
                eng.wait_ge(ks_ps, g + 1)
                o = 512 * P_V
                link(eng.tensor_tensor(prod[:, :, :], ps[:, o:o + 640].rearrange("p (t n) -> p t n", t=NT),
                                       t3[:, g % 2, :, 0:TC], ALU.mult))
                link(eng.tensor_reduce(den[:, 0, :], prod[:, :, :].rearrange("p t (s c) -> p (t s) c", c=HD), AX_X, ALU.add))
                fq = ratio_of(g, 0, NH)

                def by_head(k):
                    return den[:, k, :].rearrange("p (t a h) -> p t a h", t=NT, a=2)

                link(eng.tensor_tensor(by_head(1), by_head(0), fq, ALU.mult))
                link(eng.tensor_scalar(den[:, 2, :], den[:, 1, :], EPS, None, ALU.add))
                link(eng.reciprocal(den[:, 3, :], den[:, 2, :]))
                step.mark(eng.tensor_tensor(by_head(4), by_head(3), fq, ALU.mult))
                step.den = step.n

            def q_final(g):
                eng.wait_ge(dve_step, step.den)
                if g >= 1:
                    eng.wait_ge(qt_ps, g)
                r = den[:, 4, :].rearrange("p (t s) -> p t s", t=NT).unsqueeze(3).broadcast_to([128, NT, 8, HD])
                eng.tensor_tensor(q2[:, :, :].rearrange("p t (s c) -> p t s c", c=HD),
                                  t3[:, g % 2, :, 0:TC].rearrange("p t (s c) -> p t s c", c=HD), r, ALU.mult)\
                   .then_inc(q2_ready, 1)

            def add_fm(g):
                eng.wait_ge(tp_ps, g + 1)
                eng.wait_ge(y_ready, g + 1)
                eng.tensor_tensor(y[:, g, :], y[:, g, :], turn_bank(g), ALU.add).then_inc(ysum_ready, 1)

            def attended(g):
                m = NG + g
                eng.wait_ge(pj_ps, g + 1)
                eng.wait_ge(dw_ps, m - 1)
                eng.wait_ge(x1_ready, m - 1)
                for j in range(GP):
                    last = eng.scalar_tensor_tensor(padded(m)[:, j], project_bank(g)[:, PX * j:PX * j + PX]
                                                    .rearrange("p (h w) -> p h w", w=HW), projc[:, 0:1],
                                                    x2[:, g, PX * j:PX * j + PX].rearrange("p (h w) -> p h w", w=HW),
                                                    ALU.add, ALU.add)
                last.then_inc(xp_ready, 1)

            eng.wait_ge(w_in, 16)
            link(eng.tensor_scalar(sp[:, 4:5], ww("scale"), -1.0, None, ALU.mult))
            eng.tensor_tensor(sp[:, 0:1], ww("scale"), sp[:, 4:5], ALU.max).then_inc(abs_ready, 1)
            fold(0)
            eng.wait_ge(c_in, 16)
            diagonals(0).then_inc(diag_ready, 1)
            for s in range(2):
                eng.tensor_scalar(w1s[:, s, :], ww(f"w1_{s}"), ww(f"f{s}s1"), None, ALU.mult)
                last = eng.tensor_scalar(w2s[:, s, :], ww(f"w2_{s}", 64), ww(f"f{s}s2", 64), None, ALU.mult)
            last.then_inc(scaled, 1)
            eng.wait_ge(exp_ready, 1)
            eng.tensor_scalar(sp[:, 2:3], sp[:, 1:2], 1.0, None, ALU.add).then_inc(u_ready, 1)
            eng.wait_ge(u_ready, 1)
            for i in range(3):
                tap(0, i)
            link(eng.tensor_scalar(sp[:, 5:6], sp[:, 2:3], 1.0, None, ALU.subtract))
            link(eng.tensor_scalar(sp[:, 6:7], sp[:, 5:6], 0.0, None, ALU.is_equal))
            link(eng.tensor_tensor(sp[:, 5:6], sp[:, 5:6], sp[:, 6:7], ALU.add))
            link(eng.reciprocal(sp[:, 5:6], sp[:, 5:6]))
            link(eng.tensor_tensor(sp[:, 5:6], sp[:, 5:6], sp[:, 1:2], ALU.mult))
            eng.wait_ge(ln_ready, 1)
            link(eng.tensor_tensor(sp[:, 6:7], sp[:, 3:4], sp[:, 6:7], ALU.add))
            link(eng.tensor_tensor(sp[:, 6:7], sp[:, 6:7], sp[:, 5:6], ALU.mult))
            link(eng.scalar_tensor_tensor(sp[:, 7:8], ww("scale"), 0.0, sp[:, 6:7], ALU.max, ALU.add))
            link(eng.reciprocal(inv[:, :], sp[:, 7:8]))
            eng.tensor_scalar(wqks[:, :], ww("wqk"), inv[:, 0:1], None, ALU.mult)
            eng.tensor_scalar(dinv[:, :], cc("ident", 64)[:, 0:64], inv[0:64, 0:1], None, ALU.mult).then_inc(inv_ready, 1)
            eng.wait_ge(zeroed, 7)
            eng.wait_ge(vp_ps, 1)
            for a in range(2):
                p = slice(64 * a, 64 * a + 64)
                for s in range(2):
                    eng.tensor_copy(w1t[p, s, a, :], bank(3)[p, 128 * s:128 * s + 128])
                eng.tensor_copy(wv[p, a, :], bank(4)[p, 0:64])
                eng.tensor_copy(projt[p, a, :], bank(4)[p, 64:128])
            eng.tensor_copy(w2t[:, :, :], bank(3)[:, 256:384].rearrange("p (s c) -> p s c", s=2)).then_inc(blocks, 1)
            for i in range(3, len(TAPS[0])):
                tap(0, i)
            combine(0)
            eng.wait_ge(inv_ps, 1)
            for a in range(2):
                p = slice(64 * a, 64 * a + 64)
                eng.tensor_copy(wqk[p, a:a + 3:2, :], bank(5)[p, 0:128].rearrange("p (s c) -> p s c", s=2))
            link(eng.tensor_copy(bc[:, :], bank(5)[:, 128:192]))
            eng.tensor_tensor(kpad[:, 0, :], ww("pos", 49), bc[0:49, :], ALU.mult).then_inc(pos_ready, 1)
            for a in range(2):
                last = eng.tensor_scalar(etile[:, a, :], bc[:, :], EPS, None, ALU.mult)
            last.then_inc(e_ready, 1)
            link(eng.tensor_scalar(kpad[:, 1, :], ww("pos", 49), 0.0, EPS, ALU.max, ALU.add))
            link(eng.tensor_tensor(kpad[:, 2, :], kpad[:, 1, :], bc[0:49, :], ALU.mult))
            link(eng.tensor_tensor(kpad[:, 3, :], kpad[:, 2, :], kpad[:, 2, :], ALU.mult))
            link(eng.tensor_reduce(kpn[:, 0:1], kpad[:, 3, :], AX_X, ALU.add))
            link(eng.tensor_tensor(kpad[:, 4, :], kpad[:, 2, :], kpad[:, 3, :], ALU.mult))
            link(eng.tensor_tensor(kpad[:, 3, :], kpad[:, 4, :], kpad[:, 4, :], ALU.mult))
            link(eng.tensor_reduce(kpn[:, 1:2], kpad[:, 3, :], AX_X, ALU.add))
            link(eng.reciprocal(kpn[:, 1:2], kpn[:, 1:2]))
            eng.tensor_tensor(kpn[:, 3:4], kpn[:, 0:1], kpn[:, 1:2], ALU.mult).then_inc(pad_ratio, 1)
            eng.wait_ge(spread_ps, 1)
            eng.tensor_copy(rrow[:, :, :], bank(7)[0:35, 0:WR * HD].rearrange("p (y d) -> p y d", d=HD))
            eng.wait_ge(projc_ps, 1)
            eng.tensor_tensor(projc[:, :], bank(6)[:, 0:1], ww("projb"), ALU.add)
            eng.tensor_copy(pad_of[:, :, :], cc("pad_of", 96).rearrange("p (k n) -> p k n", k=2))
            residual(0)
            eng.wait_ge(pad_root, 1)
            eng.tensor_scalar(kpad[:, 5, :], kpad[:, 4, :], kpn[:, 2:3], None, ALU.mult).then_inc(pads_focused, 1)
            eng.wait_ge(pos_ps, 1)
            for t in range(NT):
                k = t // 4
                for a in range(2):
                    eng.tensor_copy(pose[:, t, a, :], bank(5)[:, 256 + 64 * k:320 + 64 * k])
            eng.wait_ge(pads_ps, 1)
            link(eng.tensor_copy(padr[:, :], bank(7)[0:96, 384:448]))
            link(eng.tensor_copy(padrhs[:, 0, :], padr[:, :]))
            for rest in ((32, 64), (64,)):
                for at in rest:
                    p = slice(at, at + 32)
                    link(eng.tensor_tensor(padr[p, :], padr[p, :], padrhs[p, 0, :], ALU.subtract))
                    link(eng.tensor_copy(padrhs[p, 0, :], padr[p, :]))
            for s in range(1, 8):
                last = eng.tensor_copy(padrhs[:, s, :], padrhs[:, 0, :])
            last.then_inc(set_up, 1)
            fold(1)
            diagonals(1)

            for n in range(1, SLOTS):
                g1, g2, c = n - 1, n - 2, n + 1 - NG
                for i in range(3):
                    tap(n, i)
                if n > MIXED:
                    residual(n - 1)
                if n >= MIXED and c < NG:
                    add_fm(c)
                if 0 <= g1 < NG:
                    k_raw(g1)
                    q_t(g1)
                if n == 2:
                    eng.wait_ge(band_matrix, 1)
                    eng.tensor_copy(tbot[32:64, :, 0:32], tband[0:32, :, 0:32])
                    eng.tensor_copy(tbot[96:128, :, 32:64], tband[0:32, :, 0:32]).then_inc(bottom_matrix, 1)
                for i in range(3, len(TAPS[n // NG])):
                    tap(n, i)
                if n >= MIXED and c < NG:
                    attended(c)
                combine(n)
                if 0 <= g2 < NG:
                    take_kv(g2)
                    q_scale(g2)
                if 0 <= g1 < NG:
                    norm2(g1)
                if 0 <= g2 < NG:
                    q_final(g2)
                if n < MIXED:
                    residual(n)
                    if 0 <= c:
                        add_fm(c)
                if 0 <= g1 < NG:
                    norm6(g1)
                    k_focus(g1)
                if n < MIXED and 0 <= c:
                    attended(c)
            residual(SLOTS - 1)


def kernel(**inputs):
    import concourse.bacc as bacc
    from concourse.bass_utils import run_bass_kernel_spmd

    f = {k.replace("L0_conv_", ""): np.ascontiguousarray(v) for k, v in inputs.items()}
    dt = f["x"].dtype
    consts, s2 = shape_constants()
    order = np.arange(C).reshape(NH, HD).T.ravel()
    w = np.zeros((128, WTOT), dt)

    def put(name, value, times=1):
        a, b = WCOL[name]
        value = value.reshape(value.shape[0], -1)
        for k in range(times):
            n = value.shape[0]
            w[n * k:n * k + n, a:a + value.shape[1]] = value
        return w[:, a:b]

    def put_twice(name, value):
        a, b = WCOL[name]
        n = value.shape[1]
        w[0:value.shape[0], a:a + n] = value
        w[0:value.shape[0], a + n:b] = value

    for s in range(2):
        put(f"dw{s}w", f[f"dw{s}_w"].reshape(C, 9), 2)
        put(f"dw{s}s", f[f"dw{s}_s"], 2)
        put(f"dw{s}b", f[f"dw{s}_b"], 2)
        put(f"f{s}b1", f[f"f{s}_b1"])
        put(f"f{s}s1", f[f"f{s}_s1"])
        put(f"f{s}b2", f[f"f{s}_b2"], 2)
        put(f"f{s}s2", f[f"f{s}_s2"])
        put_twice(f"w1_{s}", f[f"f{s}_w1"].reshape(HID, C))
        put(f"w2_{s}", f[f"f{s}_w2"].reshape(C, HID))
    put("scale", f["scale_p"].reshape(C), 2)
    put("dwcb", np.concatenate([f["dwc_b"][order[i] % HD:order[i] % HD + 1] for i in range(C)]), 2)
    put("projb", f["proj_b"], 2)
    put("dwcw", f["dwc_w"].reshape(HD, 25).T)
    put("pos", f["pos"].reshape(WR * WR, C))
    put_twice("wqk", np.concatenate([f["wq"], f["wkv"][:C]]))
    put_twice("wv", f["wkv"][C:][order])
    put_twice("proj", f["proj_w"][:, order])

    nc = bacc.Bacc("TRN2", target_bir_lowering=False, num_devices=1)
    arrays = {"in_x": f["x"], "in_weights": w, "in_consts": consts, "in_s2": s2}
    aps = [nc.dram_tensor(n, a.shape, mybir.dt.from_np(a.dtype), kind="ExternalInput").ap() for n, a in arrays.items()]
    out = nc.dram_tensor("out", f["x"].shape, F32, kind="ExternalOutput").ap()
    window_block_kernel(nc, *aps, out)
    r = run_bass_kernel_spmd(nc, [arrays], core_ids=[0])
    return r.results[0]["out"]
```

```python
from contextlib import ExitStack

import numpy as np

import concourse.bass as bass
from concourse import mybir

F32 = mybir.dt.float32
BF16 = mybir.dt.bfloat16
ALU = mybir.AluOpType
ACT = mybir.ActivationFunctionType
AX_X = mybir.AxisListType.X

B, C, HW, HID = 32, 64, 16, 128
NH, HD, WR = 4, 16, 7
PX = HW * HW
NG = 8
GP = 2
GC = GP * PX
TOK = WR * HW
NT = 5
TC = 2 * C
PITCH = HW + 1
PROWS = 2 * HW + 1
PADDED = 3 + (PROWS + 2) * PITCH
EPS = 1e-6

CONSTS = [("ident", 128), ("mask_band", 128), ("mask_bot", 128), ("head_mask", NH),
          ("win_band", 3), ("win_bot", 6), ("pos_sel", 256), ("pad_sum", 96), ("pad_of", 256), ("s1", WR * 35)]
WEIGHTS = [("dw0w", 9), ("dw0s", 1), ("dw0b", 1), ("dw1w", 9), ("dw1s", 1), ("dw1b", 1),
           ("f0b1", 1), ("f0s1", 1), ("f0b2", 1), ("f0s2", 1), ("f1b1", 1), ("f1s1", 1), ("f1b2", 1), ("f1s2", 1),
           ("scale", 1), ("dwcb", 1), ("projb", 1), ("dwcw", 16), ("pos", 64),
           ("w1_0", 128), ("w1_1", 128), ("w2_0", 128), ("w2_1", 128), ("wqk", 128), ("wv", 128), ("proj", 128)]


def columns(table):
    at, out = 0, {}
    for name, n in table:
        out[name] = (at, at + n)
        at += n
    return out, at


CCOL, CTOT = columns(CONSTS)
WCOL, WTOT = columns(WEIGHTS)


def shape_constants():
    c = np.zeros((128, CTOT), np.float32)

    def put(name):
        a, b = CCOL[name]
        return c[:, a:b]

    put("ident")[:] = np.eye(128)
    tok = np.arange(128)
    band_ok = tok < TOK
    wx = np.minimum(tok % HW // WR, 2)
    n_band = tok // HW * WR + tok % HW - WR * wx
    pair, low = tok // 64, tok % 64
    bot_ok = low >= 32
    n_bot = (low // HW - 2) * WR + tok % HW - WR * wx
    same = wx[:, None] == wx[None]
    put("mask_band")[:] = same & band_ok[:, None] & band_ok[None]
    put("mask_bot")[:] = same & bot_ok[:, None] & bot_ok[None] & (pair[:, None] == pair[None])
    put("head_mask")[:] = (tok[:, None] % C // HD) == np.arange(NH)[None]
    put("win_band")[:] = (wx[:, None] == np.arange(3)[None]) & band_ok[:, None]
    for j in range(2):
        put("win_bot")[:, 3 * j:3 * j + 3] = (wx[:, None] == np.arange(3)[None]) & (bot_ok & (pair == j))[:, None]
    for k, (n_of, ok) in enumerate([(n_band, band_ok), (n_bot, bot_ok)]):
        for p in np.flatnonzero(ok):
            put("pos_sel")[n_of[p], 128 * k + p] = 1
    n = np.arange(WR * WR)
    right, below = n % WR >= 2, n // WR >= 2
    for part in (0, 32, 64):
        for kind, padding in enumerate([right, below, right | below]):
            put("pad_sum")[0:WR * WR, part + kind] = padding
        put("pad_of")[part, 0:128] = band_ok & (wx == 2)
        put("pad_of")[part + 1, 128:256] = bot_ok & (wx < 2)
        put("pad_of")[part + 2, 128:256] = bot_ok & (wx == 2)
    s1 = put("s1").reshape(128, WR, 35)
    for dy in range(5):
        for dx in range(5):
            for y_out in range(WR):
                y_in = y_out + dy - 2
                if 0 <= y_in < WR:
                    s1[dy * 5 + dx, y_out, y_in * 5 + dx] = 1
    s2 = np.zeros((35, HW, TOK), np.float32)
    for y in range(WR):
        for dx in range(5):
            for x_out in range(HW):
                x_in = x_out + dx - 2
                if 0 <= x_in < HW and min(x_in // WR, 2) == min(x_out // WR, 2):
                    s2[y * 5 + dx, x_out, y * HW + x_in] = 1
    return c, s2.reshape(35, HW * TOK)


class Count:

    def __init__(self, sem):
        self.sem, self.n = sem, 0

    def mark(self, ins):
        ins.then_inc(self.sem, 1)
        self.n += 1
        return self.n


def window_block_kernel(nc, x, weights, consts, s2_in, out):
    PE_TAPS = [[0, 2], [0, 2]]
    TAPS = [[t for t in range(9) if t not in PE_TAPS[s]] for s in range(2)]

    x_v = x.rearrange("(g j a) c h w -> g (a c) j (h w)", j=GP, a=2)
    out_v = out.rearrange("(g j a) c h w -> g (a c) j (h w)", j=GP, a=2)

    with ExitStack() as ctx:
        def sb(name, *shape, dt=F32):
            return ctx.enter_context(nc.sbuf_tensor(name, list(shape), dt))

        def sem(name):
            return ctx.enter_context(nc.semaphore(name))

        ps = ctx.enter_context(nc.psum_tensor("ps", [128, 8 * 512], F32))

        def bank(k, n=1):
            return ps[:, 512 * k:512 * (k + n)]

        P_DW, P_H, P_QK, P_V = 0, 1, 3, 6

        cst = sb("cst", 128, CTOT)
        wts = sb("wts", 128, WTOT)

        def cc(name, p=128):
            a, b = CCOL[name]
            return cst[0:p, a:b]

        def ww(name, p=128):
            a, b = WCOL[name]
            return wts[0:p, a:b]

        ident = cc("ident")

        xin = sb("xin", 128, NG, GC)
        xp = sb("xp", 128, 2, PADDED)
        acc = sb("acc", 128, 2, PROWS * HW)
        x1 = sb("x1", 128, 2, GC)
        hid = sb("hid", 128, 2, 2, GC)
        x2 = sb("x2", 128, NG, GC)
        dwf = sb("dwf", 128, 2, 9)
        diag = sb("diag", 128, 5, 128)
        w1t = sb("w1t", 128, 2, 2, 128)
        w2t = sb("w2t", 128, 2, C)
        wqks = sb("wqks", 128, 128)
        wqk = sb("wqk_bd", 128, 4, C)
        wv = sb("wv_bd", 128, 2, C)
        projt = sb("projt", 128, 2, C)
        projc = sb("projc", 128, 1)
        sp = sb("sp", 128, 12)
        inv = sb("inv", 128, 1)
        dinv = sb("dinv", 64, 64)
        ones = sb("ones", 64, 128)
        bc = sb("bc", 128, C)
        etile = sb("etile", 128, 2, C)
        pose = sb("pose", 128, NT, C)
        kpad = sb("kpad", 49, 6, C)
        kpn = sb("kpn", 49, 4)
        padr = sb("padr", 96, C)
        padrhs = sb("padrhs", 96, 8, C, dt=BF16)
        pad_of = sb("pad_of", 96, 2, 128, dt=BF16)
        tqk = sb("tqk", 128, 2, NT, 2 * TC)
        kraw = sb("kraw", 128, NT, TC)
        sq = sb("sq", 128, NT, 2 * TC)
        t3 = sb("t3", 128, 2, NT, 2 * TC)
        s6 = sb("s6", 128, NT, 2 * TC)
        half2 = sb("half2", 128, 4 * NT, C // 2)
        nrm = sb("nrm", 128, 4, 20)
        foc = sb("foc", 128, 2, 20)
        kf = sb("kf", 128, NT, TC)
        vband = sb("vband", 128, NG, 8, C)
        vbot = sb("vbot", 128, NG, 2, C)
        vmb = sb("vmb", 128, 3, 8, C)
        vmt = sb("vmt", 128, 6, 2, C)
        kv = sb("kv", 128, 18, C)
        prod = sb("prod", 128, NT, TC)
        den = sb("den", 128, 5, 40)
        q2 = sb("q2", 128, NT, TC)
        qt = sb("qt", 128, GP, PX)
        y = sb("y", 128, NG, GC)
        w1s = y[:, NG - 1, 0:256].rearrange("p (s n) -> p s n", s=2)
        w2s = y[0:64, NG - 1, 256:512].rearrange("p (s n) -> p s n", s=2)
        rrow = sb("rrow", 35, WR, HD)
        tband = sb("tband", TOK, HD, TOK)
        tbot = sb("tbot", 128, HD, 128)
        fmband = sb("fmband", TOK, NG * 8, C)
        fmbot = sb("fmbot", 128, NG * 2, C)
        s2 = fmband[0:35, 0:HW * TOK // C, :].rearrange("p s c -> p (s c)")

        w_in, c_in, s2_arrived = sem("w_in"), sem("c_in"), sem("s2_arrived")
        x_in = [sem(f"x_in{g}") for g in range(NG)]
        zeroed = sem("zeroed")
        xp_ready, dw_ps, x1_ready = sem("xp_ready"), sem("dw_ps"), sem("x1_ready")
        h_ps, h_ready, f_ps, res_ready = sem("h_ps"), sem("h_ready"), sem("f_ps"), sem("res_ready")
        qk_ps, v_ps, tq_ready, kraw_ready, tk_ready = sem("qk_ps"), sem("v_ps"), sem("tq_ready"), sem("kraw_ready"), sem("tk_ready")
        krelu_ready = sem("krelu_ready")
        half2_ready, half6_ready = sem("half2_ready"), sem("half6_ready")
        sq_ready, t3_ready, s6_ready = sem("sq_ready"), sem("t3_ready"), sem("s6_ready")
        ratio_ready, foc_ready, kf_ready = sem("ratio_ready"), sem("foc_ready"), sem("kf_ready")
        v_ready, vm_ready = sem("v_ready"), sem("vm_ready")
        kv_ps, kv_ready, ks_ps, prod_ready, q2_ready = sem("kv_ps"), sem("kv_ready"), sem("ks_ps"), sem("prod_ready"), sem("q2_ready")
        qt_ps, qt_ready, y_ps, y_ready = sem("qt_ps"), sem("qt_ready"), sem("y_ps"), sem("y_ready")
        fm_ps, fm_ready = sem("fm_ps"), sem("fm_ready")
        tp_ps, ysum_ready, pj_ps = sem("tp_ps"), sem("ysum_ready"), sem("pj_ps")
        stored = sem("stored")
        exp_ready, ln_ready, pad_root, band_matrix = sem("exp_ready"), sem("ln_ready"), sem("pad_root"), sem("band_matrix")
        ffn_ps, vp_ps, spread_ps, projc_ps, inv_ps = sem("ffn_ps"), sem("vp_ps"), sem("spread_ps"), sem("projc_ps"), sem("inv_ps")
        pos_ps, pads_ps, matrix_ps = sem("pos_ps"), sem("pads_ps"), sem("matrix_ps")
        folded, acc_started = sem("folded"), sem("acc_started")
        rows_ready, pos_read, projc_read = sem("rows_ready"), sem("pos_read"), sem("projc_read")
        abs_ready, u_ready, scaled, diag_ready, blocks = sem("abs_ready"), sem("u_ready"), sem("scaled"), sem("diag_ready"), sem("blocks")
        inv_ready, pos_ready, spread_ready, e_ready = sem("inv_ready"), sem("pos_ready"), sem("spread_ready"), sem("e_ready")
        pad_ratio, pads_focused, set_up, bottom_matrix = sem("pad_ratio"), sem("pads_focused"), sem("set_up"), sem("bottom_matrix")
        dve_step = sem("dve_step")

        FM_SLOTS = {4: [0], 5: [1, 2], 6: [3, 4], 8: [5], 9: [6, 7], 10: [8, 9]}
        MATRIX_BANK = [6, 7, 1, 2]
        FM_BANK = [1, 1, 2, 1, 2, 1, 1, 2, 3, 4]
        MIXED = NG + 4
        SLOTS = 2 * NG
        AHEAD = 4

        def chunks_before(n):
            return sum(len(chunks) for slot, chunks in FM_SLOTS.items() if slot < n)

        def dw_bank(m):
            return bank(7 if m >= MIXED and m % 2 == 0 else P_DW)

        def turn_bank(g):
            return bank(1 if g < 4 else 3 + g % 2)

        def project_bank(g):
            return bank(2 if g < 4 else 5 + g % 2)

        block = ctx.enter_context(nc.Block())

        def padded(m):
            v = xp[:, m % 2, 1 + PITCH:1 + PITCH + GP * (HW + 1) * PITCH]
            return v.rearrange("p (j h w) -> p j h w", j=GP, w=PITCH)[:, :, 0:HW, 0:HW]

        def tap_rows(m, tap):
            dy, dx = tap // 3 - 1, tap % 3 - 1
            at = 1 + (1 + dy) * PITCH + dx
            return xp[:, m % 2, at:at + PROWS * PITCH].rearrange("p (r w) -> p r w", w=PITCH)[:, :, 0:HW]

        def shifted(m, tap):
            dy, dx = tap // 3 - 1, tap % 3 - 1
            at = 1 + (1 + dy) * PITCH + dx
            full = xp[:, m % 2, :]
            return bass.AP(full.tensor, full.offset + at, [list(full.ap[0]), [(HW + 1) * PITCH, GP], [PITCH, HW], [1, HW]])

        @block.sync
        def _(eng):
            eng.dma_start(wts[:, :], weights).then_inc(w_in, 16)
            for g in range(NG):
                eng.dma_start(xin[:, g, :].rearrange("p (j n) -> p j n", j=GP), x_v[g]).then_inc(x_in[g], 16)
            for g in range(NG):
                eng.wait_ge(res_ready, NG + g + 1)
                eng.dma_start(out_v[g], xin[:, g, :].rearrange("p (j n) -> p j n", j=GP)).then_inc(stored, 16)
            eng.wait_ge(stored, 16 * NG)

        @block.gpsimd
        def _(eng):
            eng.memset(xp[:, :, :], 0.0).then_inc(zeroed, 1)
            eng.memset(w1t[:, :, :, :], 0.0).then_inc(zeroed, 1)
            eng.memset(wqk[:, :, :], 0.0).then_inc(zeroed, 1)
            eng.memset(wv[:, :, :], 0.0).then_inc(zeroed, 1)
            eng.memset(projt[:, :, :], 0.0).then_inc(zeroed, 1)
            eng.memset(ones[:, :], 1.0).then_inc(zeroed, 1)
            eng.memset(tbot[:, :, :], 0.0).then_inc(zeroed, 1)
            eng.wait_ge(c_in, 16)
            eng.wait_ge(e_ready, 1)
            for g in range(NG):
                eng.wait_ge(krelu_ready, g + 1)
                if g >= 2:
                    eng.wait_ge(t3_ready, g - 1)
                    eng.wait_ge(sq_ready, g - 1)
                eng.tensor_tensor(tqk[:, g % 2, :, TC:2 * TC].rearrange("p t (a c) -> p t a c", a=2),
                                  kraw[:, :, :].rearrange("p t (a c) -> p t a c", a=2),
                                  etile[:, :, :].unsqueeze(1).broadcast_to([128, NT, 2, C]), ALU.add).then_inc(tk_ready, 1)
                eng.wait_ge(sq_ready, g + 1)
                eng.wait_ge(tk_ready, g + 1)
                if g >= 2:
                    eng.wait_ge(q2_ready, g - 1)
                eng.tensor_tensor(t3[:, g % 2, :, :], sq[:, :, :], tqk[:, g % 2, :, :], ALU.mult).then_inc(t3_ready, 1)
                if g >= 1:
                    eng.wait_ge(ratio_ready, g)
                halves = sq[:, :, :].rearrange("p t (s c) -> p (t s) c", c=C)
                eng.tensor_tensor(half2[:, :, :], halves[:, :, 0:C // 2], halves[:, :, C // 2:C], ALU.add).then_inc(half2_ready, 1)
                eng.wait_ge(s6_ready, g + 1)
                halves = s6[:, :, :].rearrange("p t (s c) -> p (t s) c", c=C)
                eng.tensor_tensor(halves[:, :, 0:C // 2], halves[:, :, 0:C // 2], halves[:, :, C // 2:C], ALU.add).then_inc(half6_ready, 1)
                eng.wait_ge(v_ready, 2 * (g + 1))
                if g >= 1:
                    eng.wait_ge(kv_ps, g)
                for w in range(3):
                    eng.tensor_scalar(vmb[:, w, :, :], vband[:, g, :, :], cc("win_band")[:, w:w + 1], 0.0,
                                      ALU.mult, ALU.add)
                for w in range(6):
                    last = eng.tensor_scalar(vmt[:, w, :, :], vbot[:, g, :, :], cc("win_bot")[:, w:w + 1], 0.0,
                                             ALU.mult, ALU.add)
                last.then_inc(vm_ready, 1)

        @block.scalar
        def _(eng):
            eng.dma_start(cst[:, :], consts).then_inc(c_in, 16)
            eng.dma_start(s2[:, :], s2_in).then_inc(s2_arrived, 16)
            def pad(g):
                eng.wait_ge(x_in[g], 16)
                if g == 0:
                    eng.wait_ge(zeroed, 1)
                if g >= 2:
                    eng.wait_ge(x1_ready, g - 1)
                    eng.wait_ge(dw_ps, g - 1)
                eng.activation(padded(g), xin[:, g, :].rearrange("p (j h w) -> p j h w", j=GP, h=HW),
                               ACT.Copy).then_inc(xp_ready, 1)

            def start_acc(m):
                s = m // NG
                eng.wait_ge(xp_ready, m + 1)
                if m % NG == 0:
                    eng.wait_ge(folded, s + 1)
                if m >= 2:
                    eng.wait_ge(x1_ready, m - 1)
                k = TAPS[s][0]
                eng.activation(acc[:, m % 2, :].rearrange("p (r w) -> p r w", w=HW), tap_rows(m, k), ACT.Identity,
                               bias=ww(f"dw{s}b"), scale=dwf[:, s, k:k + 1]).then_inc(acc_started, 1)

            def hidden(m):
                s = m // NG
                for a in range(2):
                    eng.wait_ge(h_ps, 2 * m + a + 1)
                    if m >= 2 and a == 0:
                        eng.wait_ge(f_ps, m - 1)
                    eng.activation(hid[:, m % 2, a, :], bank(P_H + a), ACT.Relu,
                                   bias=ww(f"f{s}b1")).then_inc(h_ready, 1)

            def take_v(g):
                eng.wait_ge(v_ps, g + 1)
                eng.activation(vband[:, g, :, :], ps[:, 512 * P_V:512 * P_V + 512].rearrange("p (s c) -> p s c", c=C),
                               ACT.Copy).then_inc(v_ready, 1)
                eng.activation(vbot[:, g, :, :], ps[:, 512 * P_V + 512:512 * P_V + 640].rearrange("p (s c) -> p s c", c=C),
                               ACT.Copy).then_inc(v_ready, 1)

            def relu_k(g):
                eng.wait_ge(kraw_ready, g + 1)
                eng.activation(kraw[:, :, :], kraw[:, :, :], ACT.Relu).then_inc(krelu_ready, 1)

            def squares(g):
                eng.wait_ge(tq_ready, g + 1)
                eng.wait_ge(tk_ready, g + 1)
                if g >= 1:
                    eng.wait_ge(ratio_ready, g)
                eng.activation(sq[:, :, :], tqk[:, g % 2, :, :], ACT.Square).then_inc(sq_ready, 1)

            def sixth(g):
                eng.wait_ge(t3_ready, g + 1)
                if g >= 1:
                    eng.wait_ge(ratio_ready, g)
                eng.activation(s6[:, :, :], t3[:, g % 2, :, :], ACT.Square).then_inc(s6_ready, 1)

            def ratio(g):
                eng.wait_ge(ratio_ready, g + 1)
                eng.activation(foc[:, g % 2, :], nrm[:, 3, :], ACT.Sqrt).then_inc(foc_ready, 1)

            def take_qt(g):
                eng.wait_ge(qt_ps, g + 1)
                eng.activation(qt[:, :, :], bank(P_V).rearrange("p (j n) -> p j n", j=GP), ACT.Copy).then_inc(qt_ready, 1)

            def take_kv(g):
                eng.wait_ge(kv_ps, g + 1)
                if g >= 1:
                    eng.wait_ge(y_ps, g)
                src = ps[:, 512 * P_QK:512 * P_QK + 1536].rearrange("p (k n) -> p k n", k=3)[:, :, 0:384]
                for h in range(NH):
                    last = eng.activation(kv[:, :, :].rearrange("p (k s) c -> p k (s c)", k=3)[:, :, h:384:NH],
                                          src[:, :, h:384:NH], ACT.Copy, scale=cc("head_mask")[:, h:h + 1])
                last.then_inc(kv_ready, 1)

            def take_y(g):
                eng.wait_ge(y_ps, g + 1)
                eng.activation(y[:, g, :], bank(P_V + 1), ACT.Copy).then_inc(y_ready, 1)

            def take_fm(c):
                eng.wait_ge(fm_ps, c + 1)
                half, part = divmod(c, 5)
                if part < 4:
                    src = bank(FM_BANK[c])[0:TOK].rearrange("p (d s h) -> p s d h", d=4, h=NH)
                    dst = fmband[:, 32 * half:32 * half + 32, 16 * part:16 * part + 16]
                else:
                    src = bank(FM_BANK[c]).rearrange("p (d s h) -> p s d h", d=HD, h=NH)
                    dst = fmbot[:, 8 * half:8 * half + 8, :]
                eng.activation(dst.rearrange("p s (d h) -> p s d h", h=NH), src, ACT.Copy).then_inc(fm_ready, 1)

            def take_matrix():
                for q in range(4):
                    eng.wait_ge(matrix_ps, q + 1)
                    src = bank(MATRIX_BANK[q])[0:TOK, 0:448].rearrange("p (x y d) -> p d y x", x=4, y=WR)
                    dst = tband[:, :, :].rearrange("p d (y x) -> p d y x", x=HW)[:, :, :, 4 * q:4 * q + 4]
                    last = eng.activation(dst, src, ACT.Copy)
                last.then_inc(band_matrix, 1)

            pad(0)
            start_acc(0)
            eng.wait_ge(abs_ready, 1)
            eng.activation(sp[:, 1:2], sp[:, 0:1], ACT.Exp, scale=-1.0).then_inc(exp_ready, 1)
            eng.wait_ge(u_ready, 1)
            eng.activation(sp[:, 3:4], sp[:, 2:3], ACT.Ln).then_inc(ln_ready, 1)
            eng.wait_ge(spread_ps, 1)
            eng.activation(rrow[:, :, :], bank(7)[0:35, 0:WR * HD].rearrange("p (y d) -> p y d", d=HD),
                           ACT.Copy).then_inc(rows_ready, 1)
            pad(1)
            start_acc(1)
            take_matrix()
            for n in range(SLOTS):
                g1, g2 = n - 1, n - 2
                if 0 <= g1 < NG:
                    relu_k(g1)
                    squares(g1)
                    take_v(g1)
                if 1 <= n and n + 1 < NG:
                    pad(n + 1)
                    start_acc(n + 1)
                if 0 <= g2 < NG:
                    take_kv(g2)
                if n < 2:
                    hidden(n)
                if 0 <= g1 < NG:
                    sixth(g1)
                if NG <= n + 1 < SLOTS:
                    start_acc(n + 1)
                if n >= 2:
                    hidden(n)
                if 0 <= g2 < NG:
                    take_qt(g2)
                for c in FM_SLOTS.get(n, []):
                    take_fm(c)
                if 0 <= g1 < NG:
                    ratio(g1)
                if 0 <= g2 < NG:
                    take_y(g2)
                if n == 0:
                    eng.wait_ge(pos_ps, 1)
                    for t in range(NT):
                        k = t // 4
                        last = eng.activation(pose[:, t, :], bank(5)[:, 256 + 64 * k:320 + 64 * k], ACT.Copy)
                    last.then_inc(pos_read, 1)
                    eng.wait_ge(pad_ratio, 1)
                    eng.activation(kpn[:, 2:3], kpn[:, 3:4], ACT.Sqrt).then_inc(pad_root, 1)

        @block.tensor
        def _(eng):
            def conv(m):
                s, g = divmod(m, NG)
                eng.wait_ge(xp_ready, m + 1)
                if m == MIXED:
                    eng.wait_ge(y_ready, NG)
                elif m > MIXED:
                    eng.wait_ge(res_ready, m - 1)
                elif m >= 1:
                    eng.wait_ge(res_ready, m)
                taps = PE_TAPS[s]
                for i, tap in enumerate(taps):
                    last = eng.matmul(dw_bank(m), diag[:, 2 * s + i, :], shifted(m, tap), start=(i == 0), stop=(i == len(taps) - 1))
                last.then_inc(dw_ps, 1)

            def ffn1(m):
                s = m // NG
                eng.wait_ge(x1_ready, m + 1)
                if m >= 1:
                    eng.wait_ge(h_ready, 2 * m)
                if m > min(FM_SLOTS):
                    eng.wait_ge(fm_ready, chunks_before(m))
                if NG <= m + 1 < NG + 4:
                    eng.wait_ge(xp_ready, m + 2)
                for a in range(2):
                    eng.matmul(bank(P_H + a), w1t[:, s, a, :], x1[:, m % 2, :], start=True, stop=True).then_inc(h_ps, 1)

            def ffn2(m):
                s = m // NG
                for a in range(2):
                    eng.wait_ge(h_ready, 2 * m + a + 1)
                    last = eng.matmul(dw_bank(m)[64 * a:64 * a + 64], w2t[:, s, :], hid[:, m % 2, a, :], start=True, stop=True)
                last.then_inc(f_ps, 1)

            def by_token(g, o, w, n):
                for t in range(4):
                    at = PX * (t % 2) + TOK * (t // 2)
                    eng.matmul(ps[:, o + n * t:o + n * t + n], x2[:, g, at:at + 128], w, start=True, stop=True)
                for j in range(GP):
                    at = PX * j + PX - 64
                    last = eng.matmul(ps[64 * j:64 * j + 64, o + 4 * n:o + 5 * n], x2[:, g, at:at + 64], w,
                                      start=True, stop=True)
                return last

            def project_qk(g):
                eng.wait_ge(res_ready, g + 1)
                if g >= 2:
                    eng.wait_ge(kv_ready, g - 1)
                by_token(g, 512 * P_QK, wqk[:, :, :].rearrange("p s c -> p (s c)"), 2 * TC).then_inc(qk_ps, 1)

            def project_v(g):
                if g >= 1:
                    eng.wait_ge(prod_ready, g)
                by_token(g, 512 * P_V, wv[:, :, :].rearrange("p s c -> p (s c)"), TC).then_inc(v_ps, 1)

            def key_value(g):
                eng.wait_ge(kf_ready, g + 1)
                eng.wait_ge(vm_ready, g + 1)
                if g + 1 < NG:
                    eng.wait_ge(kraw_ready, g + 2)
                    eng.wait_ge(tq_ready, g + 2)
                for t in range(4):
                    b, j = divmod(t, 2)
                    for a in range(2):
                        o = 512 * (P_QK + j) + 192 * b
                        eng.matmul(ps[64 * a:64 * a + 64, o:o + 192], kf[:, t, 64 * a:64 * a + 64],
                                   vmb[:, :, 2 * t + a, :], start=True, stop=True)
                for a in range(2):
                    o = 512 * (P_QK + 2)
                    last = eng.matmul(ps[64 * a:64 * a + 64, o:o + 384], kf[:, 4, 64 * a:64 * a + 64],
                                      vmt[:, :, a, :], start=True, stop=True)
                last.then_inc(kv_ps, 1)

            def key_sum(g):
                eng.wait_ge(kf_ready, g + 1)
                if g == 0:
                    eng.wait_ge(set_up, 1)
                eng.wait_ge(v_ready, 2 * (g + 1))
                if g >= 1:
                    eng.wait_ge(qt_ready, g)
                    eng.wait_ge(y_ready, g)
                o = 512 * P_V
                eng.matmul(ps[:, o:o + 512], cc("mask_band"), kf[:, 0:4, :].rearrange("p t c -> p (t c)"), start=True, stop=False)
                eng.matmul(ps[:, o:o + 512], pad_of[:, 0, :], padrhs[:, :, :].rearrange("p s c -> p (s c)"),
                           start=False, stop=True)
                eng.matmul(ps[:, o + 512:o + 640], cc("mask_bot"), kf[:, 4, :], start=True, stop=False)
                eng.matmul(ps[:, o + 512:o + 640], pad_of[:, 1, :],
                           padrhs[:, 0:2, :].rearrange("p s c -> p (s c)"), start=False, stop=True).then_inc(ks_ps, 1)

            def turn_q(g):
                eng.wait_ge(q2_ready, g + 1)
                eng.wait_ge(v_ready, 2 * min(g + 2, NG))
                v = bank(P_V).rearrange("p (j n) -> p j n", j=GP)
                eng.transpose(v[:, :, PX - 64:PX], q2[:, 4, :], ident)
                for t in range(4):
                    b, j = divmod(t, 2)
                    last = eng.transpose(v[:, j, TOK * b:TOK * b + TOK], q2[0:TOK, t, :], cc("ident", TOK)[:, 0:TOK])
                last.then_inc(qt_ps, 1)

            def attend(g):
                eng.wait_ge(kv_ready, g + 1)
                eng.wait_ge(qt_ready, g + 1)
                for j in range(GP):
                    for wy in range(3):
                        for wx in range(3):
                            slot = 8 * 0 + (6 * j + 3 * wy + wx if wy < 2 else 12 + 3 * j + wx)
                            ry, rx = slice(WR * wy, min(WR * wy + WR, HW)), slice(WR * wx, min(WR * wx + WR, HW))
                            for a in range(2):
                                p = slice(64 * a, 64 * a + 64)
                                src = qt[p, j, :].rearrange("p (h w) -> p h w", w=HW)[:, ry, rx]
                                dst = ps[p, 512 * (P_V + 1) + PX * j:512 * (P_V + 1) + PX * j + PX]
                                dst = dst.rearrange("p (h w) -> p h w", w=HW)[:, ry, rx]
                                last = eng.matmul(dst, kv[p, slot, :], src, start=True, stop=True)
                last.then_inc(y_ps, 1)

            def window_conv(c):
                half, part = divmod(c, 5)
                if c == 0:
                    eng.wait_ge(bottom_matrix, 1)
                if FM_BANK[c] == 3:
                    eng.wait_ge(kv_ready, NG)
                eng.wait_ge(v_ready, 8 * (half + 1))
                gs = slice(4 * half, 4 * half + 4)
                out_ps = bank(FM_BANK[c])
                if part < 4:
                    for d in range(4):
                        dc = 4 * part + d
                        last = eng.matmul(out_ps[0:TOK, 128 * d:128 * d + 128], tband[:, dc, :],
                                          vband[0:TOK, gs, :, NH * dc:NH * dc + NH].rearrange("p g s h -> p (g s) h"),
                                          start=True, stop=True)
                else:
                    for dc in range(HD):
                        last = eng.matmul(out_ps[:, 32 * dc:32 * dc + 32], tbot[:, dc, :],
                                          vbot[:, gs, :, NH * dc:NH * dc + NH].rearrange("p g s h -> p (g s) h"),
                                          start=True, stop=True)
                last.then_inc(fm_ps, 1)

            def turn_fm(g):
                eng.wait_ge(fm_ready, chunks_before(g + NG - 1))
                eng.wait_ge(h_ready, 2 * (g + NG - 1))
                if g >= 6:
                    eng.wait_ge(ysum_ready, g - 1)
                v = turn_bank(g).rearrange("p (j n) -> p j n", j=GP)
                eng.transpose(v[:, :, PX - 64:PX], fmbot[:, 2 * g:2 * g + 2, :].rearrange("p s c -> p (s c)"), ident)
                for t in range(4):
                    b, j = divmod(t, 2)
                    s = 8 * g + 2 * t
                    last = eng.transpose(v[:, j, TOK * b:TOK * b + TOK],
                                         fmband[:, s:s + 2, :].rearrange("p s c -> p (s c)"), cc("ident", TOK)[:, 0:TOK])
                last.then_inc(tp_ps, 1)

            def project(g):
                eng.wait_ge(ysum_ready, g + 1)
                if g >= 6:
                    eng.wait_ge(xp_ready, NG + g - 1)
                eng.matmul(project_bank(g), projt[:, :, :].rearrange("p a c -> p (a c)"), y[:, g, :],
                           start=True, stop=True).then_inc(pj_ps, 1)

            eng.wait_ge(c_in, 16)
            eng.wait_ge(diag_ready, 1)
            conv(0)
            eng.wait_ge(scaled, 1)
            for s in range(2):
                eng.transpose(bank(3)[:, 128 * s:128 * s + 128], w1s[:, s, :], ident)
            for s in range(2):
                last = eng.transpose(bank(3)[:, 256 + 64 * s:320 + 64 * s], w2s[:, s, :], cc("ident", 64)[:, 0:64])
            last.then_inc(ffn_ps, 1)
            eng.transpose(bank(4)[:, 0:64], ww("wv", 64), cc("ident", 64)[:, 0:64])
            eng.transpose(bank(4)[:, 64:128], ww("proj", 64), cc("ident", 64)[:, 0:64]).then_inc(vp_ps, 1)
            for y_out in range(WR):
                last = eng.matmul(bank(7)[0:35, HD * y_out:HD * y_out + HD],
                                  cc("s1", 25)[:, 35 * y_out:35 * y_out + 35], ww("dwcw", 25), start=True, stop=True)
            last.then_inc(spread_ps, 1)
            eng.wait_ge(inv_ready, 1)
            eng.wait_ge(zeroed, 6)
            eng.transpose(bank(5)[:, 0:128], wqks[:, :], ident)
            eng.matmul(bank(5)[:, 128:192], ones[:, :], dinv[:, :], start=True, stop=True).then_inc(inv_ps, 1)
            eng.wait_ge(s2_arrived, 16)
            eng.wait_ge(rows_ready, 1)
            for q in range(4):
                for k in range(4):
                    x_out = 4 * q + k
                    last = eng.matmul(bank(MATRIX_BANK[q])[0:TOK, 112 * k:112 * k + 112], s2[:, TOK * x_out:TOK * x_out + TOK],
                                      rrow[:, :, :].rearrange("p y d -> p (y d)"), start=True, stop=True)
                last.then_inc(matrix_ps, 1)
            eng.wait_ge(blocks, 1)
            eng.matmul(bank(3)[:, 0:1], projt[:, :, :].rearrange("p a c -> p (a c)"), ww("dwcb"),
                       start=True, stop=True).then_inc(projc_ps, 1)
            eng.wait_ge(band_matrix, 1)
            ffn1(0)
            eng.wait_ge(pos_ready, 1)
            for k in range(2):
                last = eng.matmul(bank(5)[:, 256 + 64 * k:320 + 64 * k], cc("pos_sel", 49)[:, 128 * k:128 * k + 128],
                                  kpad[:, 0, :], start=True, stop=True)
            last.then_inc(pos_ps, 1)
            ffn2(0)
            for n in range(1, SLOTS):
                g1, g2, c = n - 1, n - 2, n + 1 - NG
                if n == 1:
                    eng.wait_ge(pos_read, 1)
                    eng.wait_ge(projc_read, 1)
                if 0 <= g1 < NG:
                    project_qk(g1)
                if n == 1:
                    eng.wait_ge(pads_focused, 1)
                    eng.wait_ge(h_ready, 2)
                    eng.matmul(bank(P_H)[0:96, 0:64], cc("pad_sum", 49), kpad[:, 5, :],
                               start=True, stop=True).then_inc(pads_ps, 1)
                if 0 <= g2 < NG:
                    key_sum(g2)
                if 0 <= c < NG:
                    turn_fm(c)
                conv(n)
                if 0 <= g1 < NG:
                    project_v(g1)
                if 0 <= g2 < NG:
                    key_value(g2)
                if 0 <= c < NG:
                    project(c)
                ffn1(n)
                if 0 <= g2 < NG:
                    turn_q(g2)
                ffn2(n)
                for k in FM_SLOTS.get(n, []):
                    window_conv(k)
                if 0 <= g2 < NG:
                    attend(g2)

        @block.vector
        def _(eng):
            step = Count(dve_step)

            def link(ins):
                eng.wait_ge(dve_step, step.mark(ins))

            def fold(s):
                link(eng.tensor_scalar(dwf[:, s, :], ww(f"dw{s}w"), ww(f"dw{s}s"), None, ALU.mult))
                eng.tensor_scalar(dwf[:, s, 4:5], dwf[:, s, 4:5], 1.0, None, ALU.add).then_inc(folded, 1)
                eng.wait_ge(folded, s + 1)

            def diagonals(s):
                for i, tap in enumerate(PE_TAPS[s]):
                    last = eng.tensor_scalar(diag[:, 2 * s + i, :], ident, dwf[:, s, tap:tap + 1], None, ALU.mult)
                return last

            def tap(m, i):
                s = m // NG
                k = TAPS[s][i]
                a = acc[:, m % 2, :].rearrange("p (r w) -> p r w", w=HW)
                w = dwf[:, s, k:k + 1]
                if i == 1:
                    eng.wait_ge(acc_started, m + 1)
                else:
                    eng.wait_ge(dve_step, step.last)
                step.mark(eng.scalar_tensor_tensor(a, tap_rows(m, k), w, a, ALU.mult, ALU.add))
                step.last = step.n

            def combine(m):
                eng.wait_ge(dw_ps, m + 1)
                eng.wait_ge(dve_step, step.last)
                if m >= 2:
                    eng.wait_ge(h_ps, 2 * (m - 1))
                full = acc[:, m % 2, :]
                a = bass.AP(full.tensor, full.offset, [list(full.ap[0]), [(HW + 1) * HW, GP], [1, PX]])
                eng.tensor_tensor(x1[:, m % 2, :].rearrange("p (j n) -> p j n", j=GP),
                                  dw_bank(m).rearrange("p (j n) -> p j n", j=GP), a, ALU.add).then_inc(x1_ready, 1)

            def residual(m):
                s, g = divmod(m, NG)
                eng.wait_ge(f_ps, m + 1)
                eng.wait_ge(x1_ready, m + 1)
                dst = x2[:, g, :] if s == 0 else xin[:, g, :]
                eng.scalar_tensor_tensor(dst, dw_bank(m), ww(f"f{s}b2"), x1[:, m % 2, :], ALU.add, ALU.add)\
                   .then_inc(res_ready, 1)

            def q_t(g):
                eng.wait_ge(qk_ps, g + 1)
                if g >= 2:
                    eng.wait_ge(t3_ready, g - 1)
                src = ps[:, 512 * P_QK:512 * P_QK + 1280].rearrange("p (t n) -> p t n", t=NT)
                e = etile[:, :, :].rearrange("p a c -> p (a c)").unsqueeze(1).broadcast_to([128, NT, TC])
                eng.scalar_tensor_tensor(tqk[:, g % 2, :, 0:TC], src[:, :, 0:TC], 0.0, e, ALU.max, ALU.add)\
                   .then_inc(tq_ready, 1)

            def k_raw(g):
                eng.wait_ge(qk_ps, g + 1)
                if g >= 1:
                    eng.wait_ge(tk_ready, g)
                src = ps[:, 512 * P_QK:512 * P_QK + 1280].rearrange("p (t n) -> p t n", t=NT)
                eng.tensor_tensor(kraw[:, :, :].rearrange("p t (a c) -> p t a c", a=2),
                                  src[:, :, TC:2 * TC].rearrange("p t (a c) -> p t a c", a=2),
                                  pose[:, :, :].unsqueeze(2).broadcast_to([128, NT, 2, C]), ALU.add).then_inc(kraw_ready, 1)

            def norm2(g):
                eng.wait_ge(half2_ready, g + 1)
                step.mark(eng.tensor_reduce(nrm[:, 0, :], half2[:, :, :], AX_X, ALU.add))

            def norm6(g):
                eng.wait_ge(half6_ready, g + 1)
                link(eng.tensor_reduce(nrm[:, 1, :], s6[:, :, :].rearrange("p t (s c) -> p (t s) c", c=C)[:, :, 0:C // 2], AX_X, ALU.add))
                link(eng.reciprocal(nrm[:, 2, :], nrm[:, 1, :]))
                eng.tensor_tensor(nrm[:, 3, :], nrm[:, 0, :], nrm[:, 2, :], ALU.mult).then_inc(ratio_ready, 1)

            def ratio_of(g, qk, n):
                f = foc[:, g % 2, :].rearrange("p (t s a) -> p t s a", s=2, a=2)[:, :, qk, :]
                return f.unsqueeze(3).broadcast_to([128, NT, 2, n])

            def k_focus(g):
                eng.wait_ge(foc_ready, g + 1)
                if g >= 1:
                    eng.wait_ge(kv_ps, g)
                eng.tensor_tensor(kf[:, :, :].rearrange("p t (a c) -> p t a c", a=2),
                                  t3[:, g % 2, :, TC:2 * TC].rearrange("p t (a c) -> p t a c", a=2),
                                  ratio_of(g, 1, C), ALU.mult).then_inc(kf_ready, 1)

            def q_scale(g):
                eng.wait_ge(ks_ps, g + 1)
                o = 512 * P_V
                eng.tensor_tensor(prod[:, :, :], ps[:, o:o + 640].rearrange("p (t n) -> p t n", t=NT),
                                  t3[:, g % 2, :, 0:TC], ALU.mult).then_inc(prod_ready, 1)
                eng.wait_ge(prod_ready, g + 1)
                link(eng.tensor_reduce(den[:, 0, :], prod[:, :, :].rearrange("p t (s c) -> p (t s) c", c=HD), AX_X, ALU.add))
                fq = ratio_of(g, 0, NH)

                def by_head(k):
                    return den[:, k, :].rearrange("p (t a h) -> p t a h", t=NT, a=2)

                link(eng.tensor_tensor(by_head(1), by_head(0), fq, ALU.mult))
                link(eng.tensor_scalar(den[:, 2, :], den[:, 1, :], EPS, None, ALU.add))
                link(eng.reciprocal(den[:, 3, :], den[:, 2, :]))
                step.mark(eng.tensor_tensor(by_head(4), by_head(3), fq, ALU.mult))
                step.den = step.n

            def q_final(g):
                eng.wait_ge(dve_step, step.den)
                if g >= 1:
                    eng.wait_ge(qt_ps, g)
                r = den[:, 4, :].rearrange("p (t s) -> p t s", t=NT).unsqueeze(3).broadcast_to([128, NT, 8, HD])
                eng.tensor_tensor(q2[:, :, :].rearrange("p t (s c) -> p t s c", c=HD),
                                  t3[:, g % 2, :, 0:TC].rearrange("p t (s c) -> p t s c", c=HD), r, ALU.mult)\
                   .then_inc(q2_ready, 1)

            def add_fm(g):
                eng.wait_ge(tp_ps, g + 1)
                eng.wait_ge(y_ready, g + 1)
                eng.tensor_tensor(y[:, g, :], y[:, g, :], turn_bank(g), ALU.add).then_inc(ysum_ready, 1)

            def attended(g):
                m = NG + g
                eng.wait_ge(pj_ps, g + 1)
                eng.wait_ge(dw_ps, m - 1)
                eng.wait_ge(x1_ready, m - 1)
                for j in range(GP):
                    last = eng.scalar_tensor_tensor(padded(m)[:, j], project_bank(g)[:, PX * j:PX * j + PX]
                                                    .rearrange("p (h w) -> p h w", w=HW), projc[:, 0:1],
                                                    x2[:, g, PX * j:PX * j + PX].rearrange("p (h w) -> p h w", w=HW),
                                                    ALU.add, ALU.add)
                last.then_inc(xp_ready, 1)

            eng.wait_ge(w_in, 16)
            link(eng.tensor_scalar(sp[:, 4:5], ww("scale"), -1.0, None, ALU.mult))
            eng.tensor_tensor(sp[:, 0:1], ww("scale"), sp[:, 4:5], ALU.max).then_inc(abs_ready, 1)
            fold(0)
            eng.wait_ge(c_in, 16)
            diagonals(0).then_inc(diag_ready, 1)
            for s in range(2):
                eng.tensor_scalar(w1s[:, s, :], ww(f"w1_{s}"), ww(f"f{s}s1"), None, ALU.mult)
                last = eng.tensor_scalar(w2s[:, s, :], ww(f"w2_{s}", 64), ww(f"f{s}s2", 64), None, ALU.mult)
            last.then_inc(scaled, 1)
            eng.wait_ge(exp_ready, 1)
            eng.tensor_scalar(sp[:, 2:3], sp[:, 1:2], 1.0, None, ALU.add).then_inc(u_ready, 1)
            eng.wait_ge(u_ready, 1)
            for i in range(1, 3):
                tap(0, i)
            link(eng.tensor_scalar(sp[:, 5:6], sp[:, 2:3], 1.0, None, ALU.subtract))
            link(eng.tensor_scalar(sp[:, 6:7], sp[:, 5:6], 0.0, None, ALU.is_equal))
            link(eng.tensor_tensor(sp[:, 5:6], sp[:, 5:6], sp[:, 6:7], ALU.add))
            link(eng.reciprocal(sp[:, 5:6], sp[:, 5:6]))
            link(eng.tensor_tensor(sp[:, 5:6], sp[:, 5:6], sp[:, 1:2], ALU.mult))
            eng.wait_ge(ln_ready, 1)
            link(eng.tensor_tensor(sp[:, 6:7], sp[:, 3:4], sp[:, 6:7], ALU.add))
            link(eng.tensor_tensor(sp[:, 6:7], sp[:, 6:7], sp[:, 5:6], ALU.mult))
            link(eng.scalar_tensor_tensor(sp[:, 7:8], ww("scale"), 0.0, sp[:, 6:7], ALU.max, ALU.add))
            link(eng.reciprocal(inv[:, :], sp[:, 7:8]))
            eng.tensor_scalar(wqks[:, :], ww("wqk"), inv[:, 0:1], None, ALU.mult)
            eng.tensor_scalar(dinv[:, :], cc("ident", 64)[:, 0:64], inv[0:64, 0:1], None, ALU.mult).then_inc(inv_ready, 1)
            eng.wait_ge(zeroed, 7)
            eng.wait_ge(vp_ps, 1)
            for a in range(2):
                p = slice(64 * a, 64 * a + 64)
                for s in range(2):
                    eng.tensor_copy(w1t[p, s, a, :], bank(3)[p, 128 * s:128 * s + 128])
                eng.tensor_copy(wv[p, a, :], bank(4)[p, 0:64])
                eng.tensor_copy(projt[p, a, :], bank(4)[p, 64:128])
            eng.tensor_copy(w2t[:, :, :], bank(3)[:, 256:384].rearrange("p (s c) -> p s c", s=2)).then_inc(blocks, 1)
            for i in range(3, len(TAPS[0])):
                tap(0, i)
            combine(0)
            eng.wait_ge(inv_ps, 1)
            for a in range(2):
                p = slice(64 * a, 64 * a + 64)
                eng.tensor_copy(wqk[p, a:a + 3:2, :], bank(5)[p, 0:128].rearrange("p (s c) -> p s c", s=2))
            link(eng.tensor_copy(bc[:, :], bank(5)[:, 128:192]))
            eng.tensor_tensor(kpad[:, 0, :], ww("pos", 49), bc[0:49, :], ALU.mult).then_inc(pos_ready, 1)
            for a in range(2):
                last = eng.tensor_scalar(etile[:, a, :], bc[:, :], EPS, None, ALU.mult)
            last.then_inc(e_ready, 1)
            for i in range(1, 2):
                tap(1, i)
            link(eng.tensor_scalar(kpad[:, 1, :], ww("pos", 49), 0.0, EPS, ALU.max, ALU.add))
            link(eng.tensor_tensor(kpad[:, 2, :], kpad[:, 1, :], bc[0:49, :], ALU.mult))
            link(eng.tensor_tensor(kpad[:, 3, :], kpad[:, 2, :], kpad[:, 2, :], ALU.mult))
            link(eng.tensor_reduce(kpn[:, 0:1], kpad[:, 3, :], AX_X, ALU.add))
            link(eng.tensor_tensor(kpad[:, 4, :], kpad[:, 2, :], kpad[:, 3, :], ALU.mult))
            link(eng.tensor_tensor(kpad[:, 3, :], kpad[:, 4, :], kpad[:, 4, :], ALU.mult))
            link(eng.tensor_reduce(kpn[:, 1:2], kpad[:, 3, :], AX_X, ALU.add))
            link(eng.reciprocal(kpn[:, 1:2], kpn[:, 1:2]))
            eng.tensor_tensor(kpn[:, 3:4], kpn[:, 0:1], kpn[:, 1:2], ALU.mult).then_inc(pad_ratio, 1)
            eng.wait_ge(projc_ps, 1)
            eng.tensor_tensor(projc[:, :], bank(3)[:, 0:1], ww("projb"), ALU.add).then_inc(projc_read, 1)
            residual(0)
            eng.wait_ge(pad_root, 1)
            eng.tensor_scalar(kpad[:, 5, :], kpad[:, 4, :], kpn[:, 2:3], None, ALU.mult).then_inc(pads_focused, 1)
            for i in range(2, AHEAD):
                tap(1, i)

            def pads():
                eng.tensor_copy(pad_of[:, :, :], cc("pad_of", 96).rearrange("p (k n) -> p k n", k=2))
                link(eng.tensor_copy(padrhs[:, 0, :], padr[:, :]))
                for rest in ((32, 64), (64,)):
                    for at in rest:
                        p = slice(at, at + 32)
                        link(eng.tensor_tensor(padr[p, :], padr[p, :], padrhs[p, 0, :], ALU.subtract))
                        link(eng.tensor_copy(padrhs[p, 0, :], padr[p, :]))
                for s in range(1, 8):
                    last = eng.tensor_copy(padrhs[:, s, :], padrhs[:, 0, :])
                last.then_inc(set_up, 1)

            for n in range(1, SLOTS):
                g1, g2, c = n - 1, n - 2, n + 1 - NG
                taps = len(TAPS[n // NG])
                ahead = list(range(1, AHEAD)) if n + 1 < SLOTS else []
                if n > MIXED:
                    residual(n - 1)
                if 0 <= c < NG:
                    add_fm(c)
                if 0 <= g1 < NG:
                    k_raw(g1)
                    q_t(g1)
                if n == 2:
                    eng.wait_ge(band_matrix, 1)
                    eng.tensor_copy(tbot[32:64, :, 32:64], tband[0:32, :, 0:32])
                    eng.tensor_copy(tbot[96:128, :, 96:128], tband[0:32, :, 0:32]).then_inc(bottom_matrix, 1)
                if 0 <= g2 < NG:
                    q_scale(g2)
                for i in range(AHEAD, taps):
                    tap(n, i)
                if 0 <= c < NG:
                    attended(c)
                if n == 1:
                    eng.wait_ge(pads_ps, 1)
                    link(eng.tensor_copy(padr[:, :], bank(P_H)[0:96, 0:64]))
                combine(n)
                if n == 1:
                    pads()
                if n == 3:
                    fold(1)
                    diagonals(1)
                if 0 <= g2 < NG:
                    q_final(g2)
                if 0 <= g1 < NG:
                    norm2(g1)
                for i in ahead[0:2]:
                    tap(n + 1, i)
                if 0 <= g1 < NG:
                    norm6(g1)
                if n < MIXED:
                    residual(n)
                for i in ahead[2:]:
                    tap(n + 1, i)
                if 0 <= g1 < NG:
                    k_focus(g1)
            residual(SLOTS - 1)


def kernel(**inputs):
    import concourse.bacc as bacc
    from concourse.bass_utils import run_bass_kernel_spmd

    f = {k.replace("L0_conv_", ""): np.ascontiguousarray(v) for k, v in inputs.items()}
    dt = f["x"].dtype
    consts, s2 = shape_constants()
    order = np.arange(C).reshape(NH, HD).T.ravel()
    w = np.zeros((128, WTOT), dt)

    def put(name, value, times=1):
        a, b = WCOL[name]
        value = value.reshape(value.shape[0], -1)
        for k in range(times):
            n = value.shape[0]
            w[n * k:n * k + n, a:a + value.shape[1]] = value
        return w[:, a:b]

    def put_twice(name, value):
        a, b = WCOL[name]
        n = value.shape[1]
        w[0:value.shape[0], a:a + n] = value
        w[0:value.shape[0], a + n:b] = value

    for s in range(2):
        put(f"dw{s}w", f[f"dw{s}_w"].reshape(C, 9), 2)
        put(f"dw{s}s", f[f"dw{s}_s"], 2)
        put(f"dw{s}b", f[f"dw{s}_b"], 2)
        put(f"f{s}b1", f[f"f{s}_b1"])
        put(f"f{s}s1", f[f"f{s}_s1"])
        put(f"f{s}b2", f[f"f{s}_b2"], 2)
        put(f"f{s}s2", f[f"f{s}_s2"])
        put_twice(f"w1_{s}", f[f"f{s}_w1"].reshape(HID, C))
        put(f"w2_{s}", f[f"f{s}_w2"].reshape(C, HID))
    put("scale", f["scale_p"].reshape(C), 2)
    put("dwcb", np.concatenate([f["dwc_b"][order[i] % HD:order[i] % HD + 1] for i in range(C)]), 2)
    put("projb", f["proj_b"], 2)
    put("dwcw", f["dwc_w"].reshape(HD, 25).T)
    put("pos", f["pos"].reshape(WR * WR, C))
    put_twice("wqk", np.concatenate([f["wq"], f["wkv"][:C]]))
    put_twice("wv", f["wkv"][C:][order])
    put_twice("proj", f["proj_w"][:, order])

    nc = bacc.Bacc("TRN2", target_bir_lowering=False, num_devices=1)
    arrays = {"in_x": f["x"], "in_weights": w, "in_consts": consts, "in_s2": s2}
    aps = [nc.dram_tensor(n, a.shape, mybir.dt.from_np(a.dtype), kind="ExternalInput").ap() for n, a in arrays.items()]
    out = nc.dram_tensor("out", f["x"].shape, F32, kind="ExternalOutput").ap()
    window_block_kernel(nc, *aps, out)
    r = run_bass_kernel_spmd(nc, [arrays], core_ids=[0])
    return r.results[0]["out"]
```

```python
from contextlib import ExitStack

import numpy as np

import concourse.bass as bass
from concourse import mybir

F32 = mybir.dt.float32
BF16 = mybir.dt.bfloat16
ALU = mybir.AluOpType
ACT = mybir.ActivationFunctionType
AX_X = mybir.AxisListType.X

B, C, HW, HID = 32, 64, 16, 128
NH, HD, WR = 4, 16, 7
PX = HW * HW
NG = 8
GP = 2
GC = GP * PX
TOK = WR * HW
NT = 5
TC = 2 * C
PITCH = HW + 1
PROWS = 2 * HW + 1
PADDED = 3 + (PROWS + 2) * PITCH
EPS = 1e-6

CONSTS = [("ident", 128), ("mask_band", 128), ("mask_bot", 128), ("head_mask", NH),
          ("win_band", 3), ("win_bot", 6), ("pos_sel", 256), ("pad_sum", 96), ("pad_of", 256), ("s1", WR * 35)]
WEIGHTS = [("dw0w", 9), ("dw0s", 1), ("dw0b", 1), ("dw1w", 9), ("dw1s", 1), ("dw1b", 1),
           ("f0b1", 1), ("f0s1", 1), ("f0b2", 1), ("f0s2", 1), ("f1b1", 1), ("f1s1", 1), ("f1b2", 1), ("f1s2", 1),
           ("scale", 1), ("dwcb", 1), ("projb", 1), ("dwcw", 16), ("pos", 64),
           ("w1_0", 128), ("w1_1", 128), ("w2_0", 128), ("w2_1", 128), ("wqk", 128), ("wv", 128), ("proj", 128)]


def columns(table):
    at, out = 0, {}
    for name, n in table:
        out[name] = (at, at + n)
        at += n
    return out, at


CCOL, CTOT = columns(CONSTS)
WCOL, WTOT = columns(WEIGHTS)


def shape_constants():
    c = np.zeros((128, CTOT), np.float32)

    def put(name):
        a, b = CCOL[name]
        return c[:, a:b]

    put("ident")[:] = np.eye(128)
    tok = np.arange(128)
    band_ok = tok < TOK
    wx = np.minimum(tok % HW // WR, 2)
    n_band = tok // HW * WR + tok % HW - WR * wx
    pair, low = tok // 64, tok % 64
    bot_ok = low >= 32
    n_bot = (low // HW - 2) * WR + tok % HW - WR * wx
    same = wx[:, None] == wx[None]
    put("mask_band")[:] = same & band_ok[:, None] & band_ok[None]
    put("mask_bot")[:] = same & bot_ok[:, None] & bot_ok[None] & (pair[:, None] == pair[None])
    put("head_mask")[:] = (tok[:, None] % C // HD) == np.arange(NH)[None]
    put("win_band")[:] = (wx[:, None] == np.arange(3)[None]) & band_ok[:, None]
    for j in range(2):
        put("win_bot")[:, 3 * j:3 * j + 3] = (wx[:, None] == np.arange(3)[None]) & (bot_ok & (pair == j))[:, None]
    for k, (n_of, ok) in enumerate([(n_band, band_ok), (n_bot, bot_ok)]):
        for p in np.flatnonzero(ok):
            put("pos_sel")[n_of[p], 128 * k + p] = 1
    n = np.arange(WR * WR)
    right, below = n % WR >= 2, n // WR >= 2
    for part in (0, 32, 64):
        for kind, padding in enumerate([right, below, right | below]):
            put("pad_sum")[0:WR * WR, part + kind] = padding
        put("pad_of")[part, 0:128] = band_ok & (wx == 2)
        put("pad_of")[part + 1, 128:256] = bot_ok & (wx < 2)
        put("pad_of")[part + 2, 128:256] = bot_ok & (wx == 2)
    s1 = put("s1").reshape(128, WR, 35)
    for dy in range(5):
        for dx in range(5):
            for y_out in range(WR):
                y_in = y_out + dy - 2
                if 0 <= y_in < WR:
                    s1[dy * 5 + dx, y_out, y_in * 5 + dx] = 1
    s2 = np.zeros((35, HW, TOK), np.float32)
    for y in range(WR):
        for dx in range(5):
            for x_out in range(HW):
                x_in = x_out + dx - 2
                if 0 <= x_in < HW and min(x_in // WR, 2) == min(x_out // WR, 2):
                    s2[y * 5 + dx, x_out, y * HW + x_in] = 1
    return c, s2.reshape(35, HW * TOK)


class Count:

    def __init__(self, sem):
        self.sem, self.n = sem, 0

    def mark(self, ins):
        ins.then_inc(self.sem, 1)
        self.n += 1
        return self.n


def window_block_kernel(nc, x, weights, consts, s2_in, out):
    TAP_ORDER = [0, 2, 6, 8]
    PE_TAPS = [TAP_ORDER[:k] for k in (2, 3, 1, 1, 1, 2, 1, 1, 3, 3, 1, 2, 3, 3, 3, 3)]
    TAPS = [[t for t in range(9) if t not in PE_TAPS[m]] for m in range(2 * NG)]
    POOLED = [3, 4, 10, 11]

    def first_on_vector(m):
        return 2 if m in POOLED else 1

    MOST = [max(map(len, PE_TAPS[:NG])), max(map(len, PE_TAPS[NG:]))]

    x_v = x.rearrange("(g j a) c h w -> g (a c) j (h w)", j=GP, a=2)
    out_v = out.rearrange("(g j a) c h w -> g (a c) j (h w)", j=GP, a=2)

    with ExitStack() as ctx:
        def sb(name, *shape, dt=F32):
            return ctx.enter_context(nc.sbuf_tensor(name, list(shape), dt))

        def sem(name):
            return ctx.enter_context(nc.semaphore(name))

        ps = ctx.enter_context(nc.psum_tensor("ps", [128, 8 * 512], F32))

        def bank(k, n=1):
            return ps[:, 512 * k:512 * (k + n)]

        P_DW, P_H, P_QK, P_V = 0, 1, 3, 6

        cst = sb("cst", 128, CTOT)
        wts = sb("wts", 128, WTOT)

        def cc(name, p=128):
            a, b = CCOL[name]
            return cst[0:p, a:b]

        def ww(name, p=128):
            a, b = WCOL[name]
            return wts[0:p, a:b]

        ident = cc("ident")

        xin = sb("xin", 128, NG, GC)
        xp = sb("xp", 128, 2, PADDED)
        acc = sb("acc", 128, 2, PROWS * HW)
        x1 = sb("x1", 128, 2, GC)
        hid = sb("hid", 128, 2, 2, GC)
        x2 = sb("x2", 128, NG, GC)
        dwf = sb("dwf", 128, 2, 9)
        diag = sb("diag", 128, sum(MOST), 128)
        w1t = sb("w1t", 128, 2, 2, 128)
        w2t = sb("w2t", 128, 2, C)
        wqks = sb("wqks", 128, 128)
        wqk = sb("wqk_bd", 128, 4, C)
        wv = sb("wv_bd", 128, 2, C)
        projt = sb("projt", 128, 2, C)
        projc = sb("projc", 128, 1)
        sp = sb("sp", 128, 12)
        inv = sb("inv", 128, 1)
        dinv = sb("dinv", 64, 64)
        ones = sb("ones", 64, 128)
        bc = sb("bc", 128, C)
        etile = sb("etile", 128, 2, C)
        pose = sb("pose", 128, NT, C)
        kpad = sb("kpad", 49, 6, C)
        kpn = sb("kpn", 49, 4)
        padr = sb("padr", 96, C)
        padrhs = sb("padrhs", 96, 8, C, dt=BF16)
        pad_of = sb("pad_of", 96, 2, 128, dt=BF16)
        tqk = sb("tqk", 128, 2, NT, 2 * TC)
        kraw = sb("kraw", 128, NT, TC)
        sq = sb("sq", 128, NT, 2 * TC)
        t3 = sb("t3", 128, 2, NT, 2 * TC)
        s6 = sb("s6", 128, NT, 2 * TC)
        half2 = sb("half2", 128, 4 * NT, C // 2)
        nrm = sb("nrm", 128, 4, 20)
        foc = sb("foc", 128, 2, 20)
        kf = sb("kf", 128, NT, TC)
        vband = sb("vband", 128, NG, 8, C)
        vbot = sb("vbot", 128, NG, 2, C)
        vmb = sb("vmb", 128, 3, 8, C)
        vmt = sb("vmt", 128, 6, 2, C)
        kv = sb("kv", 128, 18, C)
        tapx = sb("tapx", 128, PROWS * HW)
        den = sb("den", 128, 5, 40)
        q2 = sb("q2", 128, NT, TC)
        qt = sb("qt", 128, GP, PX)
        y = sb("y", 128, NG, GC)
        w1s = y[:, NG - 1, 0:256].rearrange("p (s n) -> p s n", s=2)
        w2s = y[0:64, NG - 1, 256:512].rearrange("p (s n) -> p s n", s=2)
        rrow = sb("rrow", 35, WR, HD)
        tband = sb("tband", TOK, HD, TOK)
        tbot = sb("tbot", 128, HD, 128)
        fmband = sb("fmband", TOK, NG * 8, C)
        fmbot = sb("fmbot", 128, NG * 2, C)
        s2 = fmband[0:35, 0:HW * TOK // C, :].rearrange("p s c -> p (s c)")

        w_in, c_in, s2_arrived = sem("w_in"), sem("c_in"), sem("s2_arrived")
        x_in = [sem(f"x_in{g}") for g in range(NG)]
        zeroed = sem("zeroed")
        xp_ready, dw_ps, x1_ready = sem("xp_ready"), sem("dw_ps"), sem("x1_ready")
        h_ps, h_ready, f_ps, res_ready = sem("h_ps"), sem("h_ready"), sem("f_ps"), sem("res_ready")
        qk_ps, v_ps, tq_ready, kraw_ready, tk_ready = sem("qk_ps"), sem("v_ps"), sem("tq_ready"), sem("kraw_ready"), sem("tk_ready")
        half2_ready, half6_ready = sem("half2_ready"), sem("half6_ready")
        sq_ready, t3_ready, s6_ready = sem("sq_ready"), sem("t3_ready"), sem("s6_ready")
        ratio_ready, foc_ready, kf_ready = sem("ratio_ready"), sem("foc_ready"), sem("kf_ready")
        v_ready, vm_ready = sem("v_ready"), sem("vm_ready")
        kv_ps, kv_ready, ks_ps, prod_ready, q2_ready = sem("kv_ps"), sem("kv_ready"), sem("ks_ps"), sem("prod_ready"), sem("q2_ready")
        qt_ps, qt_ready, y_ps, y_ready = sem("qt_ps"), sem("qt_ready"), sem("y_ps"), sem("y_ready")
        fm_ps, fm_ready = sem("fm_ps"), sem("fm_ready")
        tp_ps, ysum_ready, pj_ps = sem("tp_ps"), sem("ysum_ready"), sem("pj_ps")
        stored = sem("stored")
        exp_ready, ln_ready, pad_root, band_matrix = sem("exp_ready"), sem("ln_ready"), sem("pad_root"), sem("band_matrix")
        ffn_ps, vp_ps, spread_ps, projc_ps, inv_ps = sem("ffn_ps"), sem("vp_ps"), sem("spread_ps"), sem("projc_ps"), sem("inv_ps")
        pos_ps, pads_ps, matrix_ps = sem("pos_ps"), sem("pads_ps"), sem("matrix_ps")
        acc_added, tap_product = sem("acc_added"), sem("tap_product")
        folded, acc_started = sem("folded"), sem("acc_started")
        rows_ready, pos_read, projc_read = sem("rows_ready"), sem("pos_read"), sem("projc_read")
        abs_ready, u_ready, scaled, diag_ready, blocks = sem("abs_ready"), sem("u_ready"), sem("scaled"), sem("diag_ready"), sem("blocks")
        inv_ready, pos_ready, e_ready = sem("inv_ready"), sem("pos_ready"), sem("e_ready")
        pad_ratio, pads_focused, set_up, bottom_matrix = sem("pad_ratio"), sem("pads_focused"), sem("set_up"), sem("bottom_matrix")
        dve_step = sem("dve_step")

        FM_SLOTS = {4: [0], 5: [1, 2], 6: [3, 4], 8: [5], 9: [6, 7], 10: [8, 9]}
        MATRIX_BANK = [1, 2, 6, 7]
        FM_BANK = [1, 1, 2, 1, 2, 1, 1, 2, 3, 4]
        FM_PARTS = [2, 0, 1, 3, 4, 0, 2, 3, 1, 4]
        MIXED = NG + 2
        SLOTS = 2 * NG

        def chunk(c):
            return c // 5, FM_PARTS[c]

        def chunks_before(n):
            return sum(len(chunks) for slot, chunks in FM_SLOTS.items() if slot < n)

        def dw_bank(m):
            return bank(7 if m >= MIXED and m % 2 == 0 else P_DW)

        def turn_bank(g):
            return bank(1 if g < 4 else 3 + g % 2)

        def project_bank(g):
            return bank(2 if g < 4 else 5 + g % 2)

        block = ctx.enter_context(nc.Block())

        def padded(m):
            v = xp[:, m % 2, 1 + PITCH:1 + PITCH + GP * (HW + 1) * PITCH]
            return v.rearrange("p (j h w) -> p j h w", j=GP, w=PITCH)[:, :, 0:HW, 0:HW]

        def tap_rows(m, tap):
            dy, dx = tap // 3 - 1, tap % 3 - 1
            at = 1 + (1 + dy) * PITCH + dx
            return xp[:, m % 2, at:at + PROWS * PITCH].rearrange("p (r w) -> p r w", w=PITCH)[:, :, 0:HW]

        def shifted(m, tap):
            dy, dx = tap // 3 - 1, tap % 3 - 1
            at = 1 + (1 + dy) * PITCH + dx
            full = xp[:, m % 2, :]
            return bass.AP(full.tensor, full.offset + at, [list(full.ap[0]), [(HW + 1) * PITCH, GP], [PITCH, HW], [1, HW]])

        @block.sync
        def _(eng):
            eng.dma_start(wts[:, :], weights).then_inc(w_in, 16)
            for g in range(NG):
                eng.dma_start(xin[:, g, :].rearrange("p (j n) -> p j n", j=GP), x_v[g]).then_inc(x_in[g], 16)
            for g in range(NG):
                eng.wait_ge(res_ready, NG + g + 1)
                eng.dma_start(out_v[g], xin[:, g, :].rearrange("p (j n) -> p j n", j=GP)).then_inc(stored, 16)
            eng.wait_ge(stored, 16 * NG)

        @block.gpsimd
        def _(eng):
            eng.memset(xp[:, :, :], 0.0).then_inc(zeroed, 1)
            eng.memset(w1t[:, :, :, :], 0.0).then_inc(zeroed, 1)
            eng.memset(wqk[:, :, :], 0.0).then_inc(zeroed, 1)
            eng.memset(wv[:, :, :], 0.0).then_inc(zeroed, 1)
            eng.memset(projt[:, :, :], 0.0).then_inc(zeroed, 1)
            eng.memset(ones[:, :], 1.0).then_inc(zeroed, 1)
            eng.memset(tbot[:, :, :], 0.0).then_inc(zeroed, 1)
            eng.wait_ge(c_in, 16)

            def cubes(g):
                eng.wait_ge(sq_ready, g + 1)
                eng.wait_ge(tk_ready, g + 1)
                if g >= 2:
                    eng.wait_ge(q2_ready, g - 1)
                eng.tensor_tensor(t3[:, g % 2, :, :], sq[:, :, :], tqk[:, g % 2, :, :], ALU.mult).then_inc(t3_ready, 1)

            def halves2(g):
                if g >= 1:
                    eng.wait_ge(ratio_ready, g)
                eng.wait_ge(sq_ready, g + 1)
                halves = sq[:, :, :].rearrange("p t (s c) -> p (t s) c", c=C)
                eng.tensor_tensor(half2[:, :, :], halves[:, :, 0:C // 2], halves[:, :, C // 2:C], ALU.add).then_inc(half2_ready, 1)

            def halves6(g):
                eng.wait_ge(s6_ready, g + 1)
                halves = s6[:, :, :].rearrange("p t (s c) -> p (t s) c", c=C)
                eng.tensor_tensor(halves[:, :, 0:C // 2], halves[:, :, 0:C // 2], halves[:, :, C // 2:C], ALU.add).then_inc(half6_ready, 1)

            def mask_band(g):
                eng.wait_ge(v_ready, 2 * (g + 1))
                if g >= 1:
                    eng.wait_ge(kv_ps, g)
                for w in range(3):
                    last = eng.tensor_scalar(vmb[:, w, :, :], vband[:, g, :, :], cc("win_band")[:, w:w + 1], 0.0,
                                             ALU.mult, ALU.add)
                last.then_inc(vm_ready, 1)

            def mask_bot(g):
                eng.wait_ge(v_ready, 2 * (g + 1))
                if g >= 1:
                    eng.wait_ge(kv_ps, g)
                for w in range(6):
                    last = eng.tensor_scalar(vmt[:, w, :, :], vbot[:, g, :, :], cc("win_bot")[:, w:w + 1], 0.0,
                                             ALU.mult, ALU.add)
                last.then_inc(vm_ready, 1)

            def add_tap(m):
                eng.wait_ge(acc_started, m + 1)
                eng.wait_ge(tap_product, POOLED.index(m) + 1)
                eng.tensor_tensor(acc[:, m % 2, :], acc[:, m % 2, :], tapx[:, :], ALU.add).then_inc(acc_added, 1)

            for n in range(1, NG - 1):
                g1 = n - 1
                cubes(g1)
                halves2(g1)
                if n + 1 in POOLED:
                    add_tap(n + 1)
                halves6(g1)
                mask_bot(g1)
                mask_band(g1)
            for n in range(NG - 1, NG + 2):
                g1 = n - 1
                if g1 < NG:
                    halves2(g1)
                    cubes(g1)
                    mask_band(g1)
                    mask_bot(g1)
                if n + 1 in POOLED:
                    add_tap(n + 1)
                if g1 < NG:
                    halves6(g1)
            for n in range(NG + 2, SLOTS):
                if n + 1 in POOLED:
                    add_tap(n + 1)

        @block.scalar
        def _(eng):
            eng.dma_start(cst[:, :], consts).then_inc(c_in, 16)
            eng.dma_start(s2[:, :], s2_in).then_inc(s2_arrived, 16)

            def pad(g):
                eng.wait_ge(x_in[g], 16)
                if g == 0:
                    eng.wait_ge(zeroed, 1)
                if g >= 2:
                    eng.wait_ge(x1_ready, g - 1)
                    eng.wait_ge(dw_ps, g - 1)
                eng.activation(padded(g), xin[:, g, :].rearrange("p (j h w) -> p j h w", j=GP, h=HW),
                               ACT.Copy).then_inc(xp_ready, 1)

            def start_acc(m):
                s = m // NG
                eng.wait_ge(xp_ready, m + 1)
                if m % NG == 0:
                    eng.wait_ge(folded, s + 1)
                if m >= 2:
                    eng.wait_ge(x1_ready, m - 1)
                k = TAPS[m][0]
                eng.activation(acc[:, m % 2, :].rearrange("p (r w) -> p r w", w=HW), tap_rows(m, k), ACT.Identity,
                               bias=ww(f"dw{s}b"), scale=dwf[:, s, k:k + 1]).then_inc(acc_started, 1)
                if m in POOLED:
                    at = POOLED.index(m)
                    if at >= 1:
                        eng.wait_ge(acc_added, at)
                    k = TAPS[m][1]
                    eng.activation(tapx[:, :].rearrange("p (r w) -> p r w", w=HW), tap_rows(m, k), ACT.Copy,
                                   scale=dwf[:, s, k:k + 1]).then_inc(tap_product, 1)

            def hidden(m):
                s = m // NG
                for a in range(2):
                    eng.wait_ge(h_ps, 2 * m + a + 1)
                    if m >= 2 and a == 0:
                        eng.wait_ge(f_ps, m - 1)
                    eng.activation(hid[:, m % 2, a, :], bank(P_H + a), ACT.Relu,
                                   bias=ww(f"f{s}b1")).then_inc(h_ready, 1)

            def take_v(g):
                eng.wait_ge(v_ps, g + 1)
                eng.activation(vband[:, g, :, :], ps[:, 512 * P_V:512 * P_V + 512].rearrange("p (s c) -> p s c", c=C),
                               ACT.Copy).then_inc(v_ready, 1)
                eng.activation(vbot[:, g, :, :], ps[:, 512 * P_V + 512:512 * P_V + 640].rearrange("p (s c) -> p s c", c=C),
                               ACT.Copy).then_inc(v_ready, 1)

            def squares(g):
                eng.wait_ge(tq_ready, g + 1)
                eng.wait_ge(tk_ready, g + 1)
                if g >= 1:
                    eng.wait_ge(ratio_ready, g)
                eng.activation(sq[:, :, :], tqk[:, g % 2, :, :], ACT.Square).then_inc(sq_ready, 1)

            def sixth(g):
                eng.wait_ge(t3_ready, g + 1)
                if g >= 1:
                    eng.wait_ge(ratio_ready, g)
                eng.activation(s6[:, :, :], t3[:, g % 2, :, :], ACT.Square).then_inc(s6_ready, 1)

            def ratio(g):
                eng.wait_ge(ratio_ready, g + 1)
                eng.activation(foc[:, g % 2, :], nrm[:, 3, :], ACT.Sqrt).then_inc(foc_ready, 1)

            def take_qt(g):
                eng.wait_ge(qt_ps, g + 1)
                eng.activation(qt[:, :, :], bank(P_V).rearrange("p (j n) -> p j n", j=GP), ACT.Copy).then_inc(qt_ready, 1)

            def take_kv(g):
                eng.wait_ge(kv_ps, g + 1)
                if g >= 1:
                    eng.wait_ge(y_ps, g)
                src = ps[:, 512 * P_QK:512 * P_QK + 1536].rearrange("p (k n) -> p k n", k=3)[:, :, 0:384]
                for h in range(NH):
                    last = eng.activation(kv[:, :, :].rearrange("p (k s) c -> p k (s c)", k=3)[:, :, h:384:NH],
                                          src[:, :, h:384:NH], ACT.Copy, scale=cc("head_mask")[:, h:h + 1])
                last.then_inc(kv_ready, 1)

            def take_y(g):
                eng.wait_ge(y_ps, g + 1)
                eng.activation(y[:, g, :], bank(P_V + 1), ACT.Copy).then_inc(y_ready, 1)

            def take_fm(c):
                eng.wait_ge(fm_ps, c + 1)
                half, part = chunk(c)
                if part < 4:
                    src = bank(FM_BANK[c])[0:TOK].rearrange("p (d s h) -> p s d h", d=4, h=NH)
                    dst = fmband[:, 32 * half:32 * half + 32, 16 * part:16 * part + 16]
                else:
                    src = bank(FM_BANK[c]).rearrange("p (d s h) -> p s d h", d=HD, h=NH)
                    dst = fmbot[:, 8 * half:8 * half + 8, :]
                eng.activation(dst.rearrange("p s (d h) -> p s d h", h=NH), src, ACT.Copy).then_inc(fm_ready, 1)

            def take_matrix(qs):
                for q in qs:
                    eng.wait_ge(matrix_ps, q + 1)
                    src = bank(MATRIX_BANK[q])[0:TOK, 0:448].rearrange("p (x y d) -> p d y x", x=4, y=WR)
                    dst = tband[:, :, :].rearrange("p d (y x) -> p d y x", x=HW)[:, :, :, 4 * q:4 * q + 4]
                    eng.activation(dst, src, ACT.Copy).then_inc(band_matrix, 1)

            pad(0)
            start_acc(0)
            eng.wait_ge(abs_ready, 1)
            eng.activation(sp[:, 1:2], sp[:, 0:1], ACT.Exp, scale=-1.0).then_inc(exp_ready, 1)
            eng.wait_ge(u_ready, 1)
            eng.activation(sp[:, 3:4], sp[:, 2:3], ACT.Ln).then_inc(ln_ready, 1)
            eng.wait_ge(zeroed, 5)
            eng.wait_ge(vp_ps, 1)
            for a in range(2):
                p = slice(64 * a, 64 * a + 64)
                for s in range(2):
                    eng.activation(w1t[p, s, a, :], bank(3)[p, 128 * s:128 * s + 128], ACT.Copy)
            eng.activation(w2t[:, :, :], bank(3)[:, 256:384].rearrange("p (s c) -> p s c", s=2), ACT.Copy)
            for a in range(2):
                p = slice(64 * a, 64 * a + 64)
                eng.activation(wv[p, a, :], bank(4)[p, 0:64], ACT.Copy)
                last = eng.activation(projt[p, a, :], bank(4)[p, 64:128], ACT.Copy)
            last.then_inc(blocks, 1)
            eng.wait_ge(spread_ps, 1)
            eng.activation(rrow[:, :, :], bank(7)[0:35, 0:WR * HD].rearrange("p (y d) -> p y d", d=HD),
                           ACT.Copy).then_inc(rows_ready, 1)
            pad(1)
            start_acc(1)
            take_matrix((0, 1))
            hidden(0)
            take_matrix((2,))
            eng.wait_ge(pos_ps, 1)
            for t in range(NT):
                k = t // 4
                last = eng.activation(pose[:, t, :], bank(5)[:, 256 + 64 * k:320 + 64 * k], ACT.Copy)
            last.then_inc(pos_read, 1)
            eng.wait_ge(pad_ratio, 1)
            eng.activation(kpn[:, 2:3], kpn[:, 3:4], ACT.Sqrt).then_inc(pad_root, 1)
            take_matrix((3,))
            for n in range(1, NG - 1):
                g1, g2 = n - 1, n - 2
                squares(g1)
                take_v(g1)
                pad(n + 1)
                start_acc(n + 1)
                if 0 <= g2:
                    take_kv(g2)
                hidden(n)
                if 0 <= g2:
                    take_qt(g2)
                sixth(g1)
                for k in FM_SLOTS.get(n, []):
                    take_fm(k)
                ratio(g1)
                if 0 <= g2:
                    take_y(g2)
            for n in range(NG - 1, NG + 2):
                g1, g2 = n - 1, n - 2
                if g1 < NG:
                    squares(g1)
                    take_v(g1)
                take_kv(g2)
                start_acc(n + 1)
                hidden(n)
                take_qt(g2)
                if g1 < NG:
                    sixth(g1)
                for k in FM_SLOTS.get(n, []):
                    take_fm(k)
                take_y(g2)
                if g1 < NG:
                    ratio(g1)
            for n in range(NG + 2, SLOTS):
                if n < SLOTS - 1:
                    start_acc(n + 1)
                for k in FM_SLOTS.get(n, []):
                    take_fm(k)
                hidden(n)

        @block.tensor
        def _(eng):
            def conv(m):
                s, g = divmod(m, NG)
                eng.wait_ge(xp_ready, m + 1)
                if m in (MIXED, MIXED + 1) and m % 2 == 0:
                    eng.wait_ge(y_ready, NG)
                elif m > MIXED:
                    eng.wait_ge(res_ready, m - 1)
                elif m >= 1:
                    eng.wait_ge(res_ready, m)
                taps = PE_TAPS[m]
                for i, tap in enumerate(taps):
                    last = eng.matmul(dw_bank(m), diag[:, MOST[0] * s + i, :], shifted(m, tap), start=(i == 0), stop=(i == len(taps) - 1))
                last.then_inc(dw_ps, 1)

            def ffn1(m):
                s = m // NG
                eng.wait_ge(x1_ready, m + 1)
                if m >= 1:
                    eng.wait_ge(h_ready, 2 * m)
                if m > min(FM_SLOTS):
                    eng.wait_ge(fm_ready, chunks_before(m))
                if NG <= m + 1 < NG + 4:
                    eng.wait_ge(xp_ready, m + 2)
                for a in range(2):
                    eng.matmul(bank(P_H + a), w1t[:, s, a, :], x1[:, m % 2, :], start=True, stop=True).then_inc(h_ps, 1)

            def ffn2(m):
                s = m // NG
                for a in range(2):
                    eng.wait_ge(h_ready, 2 * m + a + 1)
                    last = eng.matmul(dw_bank(m)[64 * a:64 * a + 64], w2t[:, s, :], hid[:, m % 2, a, :], start=True, stop=True)
                last.then_inc(f_ps, 1)

            def by_token(g, o, w, n):
                for t in range(4):
                    at = PX * (t % 2) + TOK * (t // 2)
                    eng.matmul(ps[:, o + n * t:o + n * t + n], x2[:, g, at:at + 128], w, start=True, stop=True)
                for j in range(GP):
                    at = PX * j + PX - 64
                    last = eng.matmul(ps[64 * j:64 * j + 64, o + 4 * n:o + 5 * n], x2[:, g, at:at + 64], w,
                                      start=True, stop=True)
                return last

            def project_qk(g):
                if g == 0:
                    eng.wait_ge(pos_read, 1)
                    eng.wait_ge(projc_read, 1)
                eng.wait_ge(res_ready, g + 1)
                if g >= 2:
                    eng.wait_ge(kv_ready, g - 1)
                by_token(g, 512 * P_QK, wqk[:, :, :].rearrange("p s c -> p (s c)"), 2 * TC).then_inc(qk_ps, 1)

            def pad_sums():
                eng.wait_ge(pads_focused, 1)
                eng.wait_ge(h_ready, 2)
                eng.matmul(bank(P_H)[0:96, 0:64], cc("pad_sum", 49), kpad[:, 5, :], start=True, stop=True).then_inc(pads_ps, 1)

            def project_v(g):
                if g == 0:
                    eng.wait_ge(band_matrix, 4)
                else:
                    eng.wait_ge(prod_ready, g)
                by_token(g, 512 * P_V, wv[:, :, :].rearrange("p s c -> p (s c)"), TC).then_inc(v_ps, 1)

            def key_value(g):
                eng.wait_ge(kf_ready, g + 1)
                eng.wait_ge(vm_ready, 2 * (g + 1))
                if g + 1 < NG:
                    eng.wait_ge(kraw_ready, g + 2)
                    eng.wait_ge(tq_ready, g + 2)
                for t in range(4):
                    b, j = divmod(t, 2)
                    for a in range(2):
                        o = 512 * (P_QK + j) + 192 * b
                        eng.matmul(ps[64 * a:64 * a + 64, o:o + 192], kf[:, t, 64 * a:64 * a + 64],
                                   vmb[:, :, 2 * t + a, :], start=True, stop=True)
                for a in range(2):
                    o = 512 * (P_QK + 2)
                    last = eng.matmul(ps[64 * a:64 * a + 64, o:o + 384], kf[:, 4, 64 * a:64 * a + 64],
                                      vmt[:, :, a, :], start=True, stop=True)
                last.then_inc(kv_ps, 1)

            def key_sum(g):
                eng.wait_ge(kf_ready, g + 1)
                if g == 0:
                    eng.wait_ge(set_up, 1)
                eng.wait_ge(v_ready, 2 * (g + 1))
                if g >= 1:
                    eng.wait_ge(qt_ready, g)
                    eng.wait_ge(y_ready, g)
                o = 512 * P_V
                eng.matmul(ps[:, o:o + 512], cc("mask_band"), kf[:, 0:4, :].rearrange("p t c -> p (t c)"), start=True, stop=False)
                eng.matmul(ps[:, o:o + 512], pad_of[:, 0, :], padrhs[:, :, :].rearrange("p s c -> p (s c)"),
                           start=False, stop=True)
                eng.matmul(ps[:, o + 512:o + 640], cc("mask_bot"), kf[:, 4, :], start=True, stop=False)
                eng.matmul(ps[:, o + 512:o + 640], pad_of[:, 1, :],
                           padrhs[:, 0:2, :].rearrange("p s c -> p (s c)"), start=False, stop=True).then_inc(ks_ps, 1)

            def turn_q(g):
                eng.wait_ge(q2_ready, g + 1)
                eng.wait_ge(v_ready, 2 * min(g + 2, NG))
                v = bank(P_V).rearrange("p (j n) -> p j n", j=GP)
                eng.transpose(v[:, :, PX - 64:PX], q2[:, 4, :], ident)
                for t in range(4):
                    b, j = divmod(t, 2)
                    last = eng.transpose(v[:, j, TOK * b:TOK * b + TOK], q2[0:TOK, t, :], cc("ident", TOK)[:, 0:TOK])
                last.then_inc(qt_ps, 1)

            def attend(g):
                eng.wait_ge(kv_ready, g + 1)
                eng.wait_ge(qt_ready, g + 1)
                for j in range(GP):
                    for wy in range(3):
                        for wx in range(3):
                            slot = 6 * j + 3 * wy + wx if wy < 2 else 12 + 3 * j + wx
                            ry, rx = slice(WR * wy, min(WR * wy + WR, HW)), slice(WR * wx, min(WR * wx + WR, HW))
                            for a in range(2):
                                p = slice(64 * a, 64 * a + 64)
                                src = qt[p, j, :].rearrange("p (h w) -> p h w", w=HW)[:, ry, rx]
                                dst = ps[p, 512 * (P_V + 1) + PX * j:512 * (P_V + 1) + PX * j + PX]
                                dst = dst.rearrange("p (h w) -> p h w", w=HW)[:, ry, rx]
                                last = eng.matmul(dst, kv[p, slot, :], src, start=True, stop=True)
                last.then_inc(y_ps, 1)

            def window_conv(c):
                half, part = chunk(c)
                if c == 0:
                    eng.wait_ge(bottom_matrix, 1)
                if FM_BANK[c] >= 3:
                    eng.wait_ge(kv_ready, NG)
                eng.wait_ge(v_ready, 8 * (half + 1))
                gs = slice(4 * half, 4 * half + 4)
                out_ps = bank(FM_BANK[c])
                if part < 4:
                    for d in range(4):
                        dc = 4 * part + d
                        last = eng.matmul(out_ps[0:TOK, 128 * d:128 * d + 128], tband[:, dc, :],
                                          vband[0:TOK, gs, :, NH * dc:NH * dc + NH].rearrange("p g s h -> p (g s) h"),
                                          start=True, stop=True)
                else:
                    for dc in range(HD):
                        last = eng.matmul(out_ps[:, 32 * dc:32 * dc + 32], tbot[:, dc, :],
                                          vbot[:, gs, :, NH * dc:NH * dc + NH].rearrange("p g s h -> p (g s) h"),
                                          start=True, stop=True)
                last.then_inc(fm_ps, 1)

            def turn_fm(g):
                eng.wait_ge(fm_ready, chunks_before(g + NG - 1))
                eng.wait_ge(h_ready, 2 * (g + NG - 1))
                if g >= 6:
                    eng.wait_ge(ysum_ready, g - 1)
                v = turn_bank(g).rearrange("p (j n) -> p j n", j=GP)
                eng.transpose(v[:, :, PX - 64:PX], fmbot[:, 2 * g:2 * g + 2, :].rearrange("p s c -> p (s c)"), ident)
                for t in range(4):
                    b, j = divmod(t, 2)
                    s = 8 * g + 2 * t
                    last = eng.transpose(v[:, j, TOK * b:TOK * b + TOK],
                                         fmband[:, s:s + 2, :].rearrange("p s c -> p (s c)"), cc("ident", TOK)[:, 0:TOK])
                last.then_inc(tp_ps, 1)

            def project(g):
                eng.wait_ge(ysum_ready, g + 1)
                if g >= 6:
                    eng.wait_ge(xp_ready, NG + g - 1)
                eng.matmul(project_bank(g), projt[:, :, :].rearrange("p a c -> p (a c)"), y[:, g, :],
                           start=True, stop=True).then_inc(pj_ps, 1)

            eng.wait_ge(c_in, 16)
            eng.wait_ge(diag_ready, 1)
            conv(0)
            eng.wait_ge(scaled, 1)
            for s in range(2):
                eng.transpose(bank(3)[:, 128 * s:128 * s + 128], w1s[:, s, :], ident)
            for s in range(2):
                last = eng.transpose(bank(3)[:, 256 + 64 * s:320 + 64 * s], w2s[:, s, :], cc("ident", 64)[:, 0:64])
            last.then_inc(ffn_ps, 1)
            eng.transpose(bank(4)[:, 0:64], ww("wv", 64), cc("ident", 64)[:, 0:64])
            eng.transpose(bank(4)[:, 64:128], ww("proj", 64), cc("ident", 64)[:, 0:64]).then_inc(vp_ps, 1)
            for y_out in range(WR):
                last = eng.matmul(bank(7)[0:35, HD * y_out:HD * y_out + HD],
                                  cc("s1", 25)[:, 35 * y_out:35 * y_out + 35], ww("dwcw", 25), start=True, stop=True)
            last.then_inc(spread_ps, 1)
            eng.wait_ge(inv_ready, 1)
            eng.wait_ge(zeroed, 6)
            eng.transpose(bank(5)[:, 0:128], wqks[:, :], ident)
            eng.matmul(bank(5)[:, 128:192], ones[:, :], dinv[:, :], start=True, stop=True).then_inc(inv_ps, 1)
            eng.wait_ge(s2_arrived, 16)
            eng.wait_ge(rows_ready, 1)

            def matrix(q):
                for k in range(4):
                    x_out = 4 * q + k
                    last = eng.matmul(bank(MATRIX_BANK[q])[0:TOK, 112 * k:112 * k + 112], s2[:, TOK * x_out:TOK * x_out + TOK],
                                      rrow[:, :, :].rearrange("p y d -> p (y d)"), start=True, stop=True)
                last.then_inc(matrix_ps, 1)

            matrix(0)
            matrix(1)
            eng.wait_ge(blocks, 1)
            eng.matmul(bank(3)[:, 0:1], projt[:, :, :].rearrange("p a c -> p (a c)"), ww("dwcb"),
                       start=True, stop=True).then_inc(projc_ps, 1)
            eng.wait_ge(band_matrix, 2)
            ffn1(0)
            matrix(2)
            eng.wait_ge(pos_ready, 1)
            for k in range(2):
                last = eng.matmul(bank(5)[:, 256 + 64 * k:320 + 64 * k], cc("pos_sel", 49)[:, 128 * k:128 * k + 128],
                                  kpad[:, 0, :], start=True, stop=True)
            last.then_inc(pos_ps, 1)
            ffn2(0)
            matrix(3)
            for n in range(1, NG - 1):
                g1, g2 = n - 1, n - 2
                project_qk(g1)
                if n == 1:
                    pad_sums()
                if 0 <= g2:
                    key_sum(g2)
                conv(n)
                project_v(g1)
                if 0 <= g2:
                    key_value(g2)
                ffn1(n)
                if 0 <= g2:
                    turn_q(g2)
                ffn2(n)
                for k in FM_SLOTS.get(n, []):
                    window_conv(k)
                if 0 <= g2:
                    attend(g2)
            for n in range(NG - 1, NG + 2):
                g1, g2, c = n - 1, n - 2, n + 1 - NG
                if g1 < NG:
                    project_qk(g1)
                turn_fm(c)
                conv(n)
                key_sum(g2)
                if g1 < NG:
                    project_v(g1)
                project(c)
                key_value(g2)
                turn_q(g2)
                ffn1(n)
                ffn2(n)
                for k in FM_SLOTS.get(n, []):
                    window_conv(k)
                attend(g2)
            for n in range(NG + 2, SLOTS):
                c = n + 1 - NG
                if c < NG:
                    turn_fm(c)
                conv(n)
                if c < NG:
                    project(c)
                for k in FM_SLOTS.get(n, []):
                    window_conv(k)
                ffn1(n)
                ffn2(n)

        @block.vector
        def _(eng):
            step = Count(dve_step)

            def link(ins):
                eng.wait_ge(dve_step, step.mark(ins))

            def fold(s):
                link(eng.tensor_scalar(dwf[:, s, :], ww(f"dw{s}w"), ww(f"dw{s}s"), None, ALU.mult))
                eng.tensor_scalar(dwf[:, s, 4:5], dwf[:, s, 4:5], 1.0, None, ALU.add).then_inc(folded, 1)
                eng.wait_ge(folded, s + 1)

            def diagonals(s):
                for i, tap in enumerate(TAP_ORDER[:MOST[s]]):
                    last = eng.tensor_scalar(diag[:, MOST[0] * s + i, :], ident, dwf[:, s, tap:tap + 1], None, ALU.mult)
                return last

            def tap(m, i):
                s = m // NG
                k = TAPS[m][i]
                a = acc[:, m % 2, :].rearrange("p (r w) -> p r w", w=HW)
                w = dwf[:, s, k:k + 1]
                if i == first_on_vector(m):
                    if m in POOLED:
                        eng.wait_ge(acc_added, POOLED.index(m) + 1)
                    else:
                        eng.wait_ge(acc_started, m + 1)
                else:
                    eng.wait_ge(dve_step, step.last)
                step.mark(eng.scalar_tensor_tensor(a, tap_rows(m, k), w, a, ALU.mult, ALU.add))
                step.last = step.n

            done = [first_on_vector(m) for m in range(SLOTS)]
            ALL = 9

            def taps(m, count):
                if m < SLOTS:
                    for i in range(done[m], min(done[m] + count, len(TAPS[m]))):
                        tap(m, i)
                        done[m] += 1

            def combine(m):
                eng.wait_ge(dw_ps, m + 1)
                eng.wait_ge(dve_step, step.last)
                if m >= 2:
                    eng.wait_ge(h_ps, 2 * (m - 1))
                full = acc[:, m % 2, :]
                a = bass.AP(full.tensor, full.offset, [list(full.ap[0]), [(HW + 1) * HW, GP], [1, PX]])
                eng.tensor_tensor(x1[:, m % 2, :].rearrange("p (j n) -> p j n", j=GP),
                                  dw_bank(m).rearrange("p (j n) -> p j n", j=GP), a, ALU.add).then_inc(x1_ready, 1)

            def residual(m):
                s, g = divmod(m, NG)
                eng.wait_ge(f_ps, m + 1)
                eng.wait_ge(x1_ready, m + 1)
                dst = x2[:, g, :] if s == 0 else xin[:, g, :]
                eng.scalar_tensor_tensor(dst, dw_bank(m), ww(f"f{s}b2"), x1[:, m % 2, :], ALU.add, ALU.add)\
                   .then_inc(res_ready, 1)

            def q_t(g):
                eng.wait_ge(qk_ps, g + 1)
                if g >= 2:
                    eng.wait_ge(t3_ready, g - 1)
                src = ps[:, 512 * P_QK:512 * P_QK + 1280].rearrange("p (t n) -> p t n", t=NT)
                e = etile[:, :, :].rearrange("p a c -> p (a c)").unsqueeze(1).broadcast_to([128, NT, TC])
                eng.scalar_tensor_tensor(tqk[:, g % 2, :, 0:TC], src[:, :, 0:TC], 0.0, e, ALU.max, ALU.add)\
                   .then_inc(tq_ready, 1)

            def k_raw(g):
                eng.wait_ge(qk_ps, g + 1)
                if g >= 1:
                    eng.wait_ge(tk_ready, g)
                src = ps[:, 512 * P_QK:512 * P_QK + 1280].rearrange("p (t n) -> p t n", t=NT)
                eng.tensor_tensor(kraw[:, :, :].rearrange("p t (a c) -> p t a c", a=2),
                                  src[:, :, TC:2 * TC].rearrange("p t (a c) -> p t a c", a=2),
                                  pose[:, :, :].unsqueeze(2).broadcast_to([128, NT, 2, C]), ALU.add).then_inc(kraw_ready, 1)

            def k_t(g):
                eng.wait_ge(kraw_ready, g + 1)
                if g >= 2:
                    eng.wait_ge(t3_ready, g - 1)
                    eng.wait_ge(sq_ready, g - 1)
                e = etile[:, :, :].rearrange("p a c -> p (a c)").unsqueeze(1).broadcast_to([128, NT, TC])
                eng.scalar_tensor_tensor(tqk[:, g % 2, :, TC:2 * TC], kraw[:, :, :], 0.0, e, ALU.max, ALU.add)\
                   .then_inc(tk_ready, 1)

            def norm2(g):
                eng.wait_ge(half2_ready, g + 1)
                step.mark(eng.tensor_reduce(nrm[:, 0, :], half2[:, :, :], AX_X, ALU.add))

            def norm6(g):
                eng.wait_ge(half6_ready, g + 1)
                link(eng.tensor_reduce(nrm[:, 1, :], s6[:, :, :].rearrange("p t (s c) -> p (t s) c", c=C)[:, :, 0:C // 2], AX_X, ALU.add))
                link(eng.reciprocal(nrm[:, 2, :], nrm[:, 1, :]))
                eng.tensor_tensor(nrm[:, 3, :], nrm[:, 0, :], nrm[:, 2, :], ALU.mult).then_inc(ratio_ready, 1)

            def ratio_of(g, qk, n):
                f = foc[:, g % 2, :].rearrange("p (t s a) -> p t s a", s=2, a=2)[:, :, qk, :]
                return f.unsqueeze(3).broadcast_to([128, NT, 2, n])

            def k_focus(g):
                eng.wait_ge(foc_ready, g + 1)
                if g >= 1:
                    eng.wait_ge(kv_ps, g)
                eng.tensor_tensor(kf[:, :, :].rearrange("p t (a c) -> p t a c", a=2),
                                  t3[:, g % 2, :, TC:2 * TC].rearrange("p t (a c) -> p t a c", a=2),
                                  ratio_of(g, 1, C), ALU.mult).then_inc(kf_ready, 1)

            def q_dot(g):
                eng.wait_ge(ks_ps, g + 1)
                o = 512 * P_V
                eng.tensor_tensor(q2[:, :, :], ps[:, o:o + 640].rearrange("p (t n) -> p t n", t=NT),
                                  t3[:, g % 2, :, 0:TC], ALU.mult).then_inc(prod_ready, 1)

            def q_scale(g):
                eng.wait_ge(prod_ready, g + 1)
                link(eng.tensor_reduce(den[:, 0, :], q2[:, :, :].rearrange("p t (s c) -> p (t s) c", c=HD), AX_X, ALU.add))
                fq = ratio_of(g, 0, NH)

                def by_head(k):
                    return den[:, k, :].rearrange("p (t a h) -> p t a h", t=NT, a=2)

                link(eng.tensor_tensor(by_head(1), by_head(0), fq, ALU.mult))
                link(eng.tensor_scalar(den[:, 2, :], den[:, 1, :], EPS, None, ALU.add))
                link(eng.reciprocal(den[:, 3, :], den[:, 2, :]))
                step.mark(eng.tensor_tensor(by_head(4), by_head(3), fq, ALU.mult))
                step.den = step.n

            def q_final(g):
                eng.wait_ge(dve_step, step.den)
                if g >= 1:
                    eng.wait_ge(qt_ps, g)
                r = den[:, 4, :].rearrange("p (t s) -> p t s", t=NT).unsqueeze(3).broadcast_to([128, NT, 8, HD])
                eng.tensor_tensor(q2[:, :, :].rearrange("p t (s c) -> p t s c", c=HD),
                                  t3[:, g % 2, :, 0:TC].rearrange("p t (s c) -> p t s c", c=HD), r, ALU.mult)\
                   .then_inc(q2_ready, 1)

            def add_fm(g):
                eng.wait_ge(tp_ps, g + 1)
                eng.wait_ge(y_ready, g + 1)
                eng.tensor_tensor(y[:, g, :], y[:, g, :], turn_bank(g), ALU.add).then_inc(ysum_ready, 1)

            def attended(g):
                m = NG + g
                eng.wait_ge(pj_ps, g + 1)
                eng.wait_ge(dw_ps, m - 1)
                eng.wait_ge(x1_ready, m - 1)
                for j in range(GP):
                    last = eng.scalar_tensor_tensor(padded(m)[:, j], project_bank(g)[:, PX * j:PX * j + PX]
                                                    .rearrange("p (h w) -> p h w", w=HW), projc[:, 0:1],
                                                    x2[:, g, PX * j:PX * j + PX].rearrange("p (h w) -> p h w", w=HW),
                                                    ALU.add, ALU.add)
                last.then_inc(xp_ready, 1)

            eng.wait_ge(w_in, 16)
            link(eng.tensor_scalar(sp[:, 4:5], ww("scale"), -1.0, None, ALU.mult))
            eng.tensor_tensor(sp[:, 0:1], ww("scale"), sp[:, 4:5], ALU.max).then_inc(abs_ready, 1)
            fold(0)
            eng.wait_ge(c_in, 16)
            diagonals(0).then_inc(diag_ready, 1)
            for s in range(2):
                eng.tensor_scalar(w1s[:, s, :], ww(f"w1_{s}"), ww(f"f{s}s1"), None, ALU.mult)
                last = eng.tensor_scalar(w2s[:, s, :], ww(f"w2_{s}", 64), ww(f"f{s}s2", 64), None, ALU.mult)
            last.then_inc(scaled, 1)
            eng.wait_ge(exp_ready, 1)
            eng.tensor_scalar(sp[:, 2:3], sp[:, 1:2], 1.0, None, ALU.add).then_inc(u_ready, 1)
            eng.wait_ge(u_ready, 1)
            taps(0, 2)
            link(eng.tensor_scalar(sp[:, 5:6], sp[:, 2:3], 1.0, None, ALU.subtract))
            link(eng.tensor_scalar(sp[:, 6:7], sp[:, 5:6], 0.0, None, ALU.is_equal))
            link(eng.tensor_tensor(sp[:, 5:6], sp[:, 5:6], sp[:, 6:7], ALU.add))
            link(eng.reciprocal(sp[:, 5:6], sp[:, 5:6]))
            link(eng.tensor_tensor(sp[:, 5:6], sp[:, 5:6], sp[:, 1:2], ALU.mult))
            eng.wait_ge(ln_ready, 1)
            link(eng.tensor_tensor(sp[:, 6:7], sp[:, 3:4], sp[:, 6:7], ALU.add))
            link(eng.tensor_tensor(sp[:, 6:7], sp[:, 6:7], sp[:, 5:6], ALU.mult))
            link(eng.scalar_tensor_tensor(sp[:, 7:8], ww("scale"), 0.0, sp[:, 6:7], ALU.max, ALU.add))
            link(eng.reciprocal(inv[:, :], sp[:, 7:8]))
            eng.tensor_scalar(wqks[:, :], ww("wqk"), inv[:, 0:1], None, ALU.mult)
            eng.tensor_scalar(dinv[:, :], cc("ident", 64)[:, 0:64], inv[0:64, 0:1], None, ALU.mult).then_inc(inv_ready, 1)
            taps(0, ALL)
            combine(0)
            eng.wait_ge(inv_ps, 1)
            for a in range(2):
                p = slice(64 * a, 64 * a + 64)
                eng.tensor_copy(wqk[p, a:a + 3:2, :], bank(5)[p, 0:128].rearrange("p (s c) -> p s c", s=2))
            link(eng.tensor_copy(bc[:, :], bank(5)[:, 128:192]))
            eng.tensor_tensor(kpad[:, 0, :], ww("pos", 49), bc[0:49, :], ALU.mult).then_inc(pos_ready, 1)
            for a in range(2):
                last = eng.tensor_scalar(etile[:, a, :], bc[:, :], EPS, None, ALU.mult)
            last.then_inc(e_ready, 1)
            taps(1, 1)
            link(eng.tensor_scalar(kpad[:, 1, :], ww("pos", 49), 0.0, EPS, ALU.max, ALU.add))
            link(eng.tensor_tensor(kpad[:, 2, :], kpad[:, 1, :], bc[0:49, :], ALU.mult))
            link(eng.tensor_tensor(kpad[:, 3, :], kpad[:, 2, :], kpad[:, 2, :], ALU.mult))
            link(eng.tensor_reduce(kpn[:, 0:1], kpad[:, 3, :], AX_X, ALU.add))
            link(eng.tensor_tensor(kpad[:, 4, :], kpad[:, 2, :], kpad[:, 3, :], ALU.mult))
            link(eng.tensor_tensor(kpad[:, 3, :], kpad[:, 4, :], kpad[:, 4, :], ALU.mult))
            link(eng.tensor_reduce(kpn[:, 1:2], kpad[:, 3, :], AX_X, ALU.add))
            link(eng.reciprocal(kpn[:, 1:2], kpn[:, 1:2]))
            eng.tensor_tensor(kpn[:, 3:4], kpn[:, 0:1], kpn[:, 1:2], ALU.mult).then_inc(pad_ratio, 1)
            eng.wait_ge(projc_ps, 1)
            eng.tensor_tensor(projc[:, :], bank(3)[:, 0:1], ww("projb"), ALU.add).then_inc(projc_read, 1)
            taps(1, 3)
            residual(0)
            eng.wait_ge(pad_root, 1)
            eng.tensor_scalar(kpad[:, 5, :], kpad[:, 4, :], kpn[:, 2:3], None, ALU.mult).then_inc(pads_focused, 1)

            def copy_bottom_matrix():
                eng.wait_ge(band_matrix, 4)
                eng.tensor_copy(tbot[32:64, :, 32:64], tband[0:32, :, 0:32])
                eng.tensor_copy(tbot[96:128, :, 96:128], tband[0:32, :, 0:32]).then_inc(bottom_matrix, 1)

            def take_pad_sums():
                eng.wait_ge(pads_ps, 1)
                link(eng.tensor_copy(padr[:, :], bank(P_H)[0:96, 0:64]))

            def pads():
                eng.tensor_copy(pad_of[:, :, :], cc("pad_of", 96).rearrange("p (k n) -> p k n", k=2))
                link(eng.tensor_copy(padrhs[:, 0, :], padr[:, :]))
                for rest in ((32, 64), (64,)):
                    for at in rest:
                        p = slice(at, at + 32)
                        link(eng.tensor_tensor(padr[p, :], padr[p, :], padrhs[p, 0, :], ALU.subtract))
                        link(eng.tensor_copy(padrhs[p, 0, :], padr[p, :]))
                for s in range(1, 8):
                    last = eng.tensor_copy(padrhs[:, s, :], padrhs[:, 0, :])
                last.then_inc(set_up, 1)

            for n in range(1, NG - 1):
                g1, g2 = n - 1, n - 2
                k_raw(g1)
                q_t(g1)
                k_t(g1)
                if 0 <= g2:
                    q_dot(g2)
                if n == 2:
                    copy_bottom_matrix()
                taps(n, ALL)
                if n == 1:
                    take_pad_sums()
                combine(n)
                if n == 1:
                    pads()
                if n == 3:
                    fold(1)
                    diagonals(1)
                if 0 <= g2:
                    q_scale(g2)
                    q_final(g2)
                residual(n)
                taps(n + 1, 1)
                norm2(g1)
                taps(n + 1, 2)
                norm6(g1)
                taps(n + 1, 1)
                k_focus(g1)
            for n in range(NG - 1, NG + 2):
                g1, g2, c = n - 1, n - 2, n + 1 - NG
                if g1 < NG:
                    q_t(g1)
                    k_raw(g1)
                    k_t(g1)
                taps(n, 1)
                add_fm(c)
                q_dot(g2)
                q_scale(g2)
                taps(n, 1)
                attended(c)
                q_final(g2)
                taps(n, ALL)
                combine(n)
                if g1 < NG:
                    norm2(g1)
                taps(n + 1, 3)
                residual(n)
                if g1 < NG:
                    norm6(g1)
                taps(n + 1, 1)
                if g1 < NG:
                    k_focus(g1)
            for n in range(NG + 2, SLOTS):
                c = n + 1 - NG
                if n > MIXED:
                    residual(n - 1)
                if c < NG:
                    add_fm(c)
                taps(n, ALL)
                combine(n)
                if c < NG:
                    attended(c)
                taps(n + 1, 4)
            residual(SLOTS - 1)


def kernel(**inputs):
    import concourse.bacc as bacc
    from concourse.bass_utils import run_bass_kernel_spmd

    f = {k.replace("L0_conv_", ""): np.ascontiguousarray(v) for k, v in inputs.items()}
    dt = f["x"].dtype
    consts, s2 = shape_constants()
    order = np.arange(C).reshape(NH, HD).T.ravel()
    w = np.zeros((128, WTOT), dt)

    def put(name, value, times=1):
        a, b = WCOL[name]
        value = value.reshape(value.shape[0], -1)
        for k in range(times):
            n = value.shape[0]
            w[n * k:n * k + n, a:a + value.shape[1]] = value
        return w[:, a:b]

    def put_twice(name, value):
        a, b = WCOL[name]
        n = value.shape[1]
        w[0:value.shape[0], a:a + n] = value
        w[0:value.shape[0], a + n:b] = value

    for s in range(2):
        put(f"dw{s}w", f[f"dw{s}_w"].reshape(C, 9), 2)
        put(f"dw{s}s", f[f"dw{s}_s"], 2)
        put(f"dw{s}b", f[f"dw{s}_b"], 2)
        put(f"f{s}b1", f[f"f{s}_b1"])
        put(f"f{s}s1", f[f"f{s}_s1"])
        put(f"f{s}b2", f[f"f{s}_b2"], 2)
        put(f"f{s}s2", f[f"f{s}_s2"])
        put_twice(f"w1_{s}", f[f"f{s}_w1"].reshape(HID, C))
        put(f"w2_{s}", f[f"f{s}_w2"].reshape(C, HID))
    put("scale", f["scale_p"].reshape(C), 2)
    put("dwcb", np.concatenate([f["dwc_b"][order[i] % HD:order[i] % HD + 1] for i in range(C)]), 2)
    put("projb", f["proj_b"], 2)
    put("dwcw", f["dwc_w"].reshape(HD, 25).T)
    put("pos", f["pos"].reshape(WR * WR, C))
    put_twice("wqk", np.concatenate([f["wq"], f["wkv"][:C]]))
    put_twice("wv", f["wkv"][C:][order])
    put_twice("proj", f["proj_w"][:, order])

    nc = bacc.Bacc("TRN2", target_bir_lowering=False, num_devices=1)
    arrays = {"in_x": f["x"], "in_weights": w, "in_consts": consts, "in_s2": s2}
    aps = [nc.dram_tensor(n, a.shape, mybir.dt.from_np(a.dtype), kind="ExternalInput").ap() for n, a in arrays.items()]
    out = nc.dram_tensor("out", f["x"].shape, F32, kind="ExternalOutput").ap()
    window_block_kernel(nc, *aps, out)
    r = run_bass_kernel_spmd(nc, [arrays], core_ids=[0])
    return r.results[0]["out"]
```
